# Optimizing a Trainium2 kernel written in Bass

```python
import numpy as np
import jax
import jax.numpy as jnp

def _softmax(x, axis=-1):
    return jax.nn.softmax(x, axis=axis)

def _gelu(x):
    return jax.nn.gelu(x, approximate=True)

def _silu(x):
    return jax.nn.silu(x)

def _sigmoid(x):
    return jax.nn.sigmoid(x)

def _layernorm(x, axis=-1, eps=1e-05):
    m = jnp.mean(x, axis=axis, keepdims=True)
    v = jnp.var(x, axis=axis, keepdims=True)
    return (x - m) / jnp.sqrt(v + eps)

def _scatter_add(tgt, idx, src, axis=0):
    return tgt.at[idx].add(src)

def _segment_sum(src, seg, n):
    return jax.ops.segment_sum(src, seg, n)
kernel_name = 'mk_adj_preln_d4_adj_r2_0bfa85'

def setup_inputs(seed: int=0):
    np.random.seed(seed)
    _w = jnp.asarray

    def _rec_inputs():
        import jax
        import jax.numpy as jnp
        _gk = jax.random.key(seed)
        x = 7.22e-05 + 1 * jax.random.normal(jax.random.fold_in(_gk, 1), (128, 128, 256), jnp.float32)
        _a = jax.random.bernoulli(jax.random.fold_in(_gk, 2), 0.125, (128, 128))
        _a = jnp.logical_or(_a, jnp.swapaxes(_a, -1, -2))
        _a = jnp.logical_or(_a, jnp.eye(128, dtype=bool))
        _af = _a.astype(jnp.float32)
        adj = _af
        return (x, adj)
    x, adj = _rec_inputs()

    def _L0_gnn_setup():
        import jax, jax.numpy as jnp
        import numpy as np
        B, N, D = (8, 1024, 256)
        key = jax.random.key(seed)
        k1, k2, k3, k4, k5 = jax.random.split(key, 5)
        neuron_states = jax.random.normal(k1, (B, N, D), dtype=jnp.float32)
        adjacency = jax.random.randint(k2, (N, N), 0, 2).astype(jnp.float32)
        scale = 1.0 / np.sqrt(D)
        Wq = jax.random.normal(k3, (D, D), dtype=jnp.float32) * scale
        Wk = jax.random.normal(k4, (D, D), dtype=jnp.float32) * scale
        Wv = jax.random.normal(k5, (D, D), dtype=jnp.float32) * scale
        return {'neuron_states': neuron_states, 'adjacency': adjacency, 'Wq': Wq, 'Wk': Wk, 'Wv': Wv}
    _L0_gnn_all = _L0_gnn_setup()
    _L0_gnn_in = {k: v for k, v in _L0_gnn_all.items() if k in ('Wq', 'Wk', 'Wv')}
    del _L0_gnn_all

    def _L1_gnn_setup():
        import jax, jax.numpy as jnp
        import numpy as np
        B, N, D, H = (4, 1024, 256, 8)
        HD = D // H
        key = jax.random.key(seed)
        ks = jax.random.split(key, 10)
        x = jax.random.normal(ks[0], (B, N, D), dtype=jnp.float32)
        adj = (jax.random.uniform(ks[1], (N, N)) < 0.1).astype(jnp.float32)
        s = 1.0 / np.sqrt(D)
        Wq = jax.random.normal(ks[2], (D, D), dtype=jnp.float32) * s
        Wk = jax.random.normal(ks[3], (D, D), dtype=jnp.float32) * s
        Wv = jax.random.normal(ks[4], (D, D), dtype=jnp.float32) * s
        Wo = jax.random.normal(ks[5], (D, D), dtype=jnp.float32) * s
        bq = jnp.zeros((D,), jnp.float32)
        bk = jnp.zeros((D,), jnp.float32)
        bv = jnp.zeros((D,), jnp.float32)
        bo = jnp.zeros((D,), jnp.float32)
        return {'x': x, 'adj': adj, 'Wq': Wq, 'bq': bq, 'Wk': Wk, 'bk': bk, 'Wv': Wv, 'bv': bv, 'Wo': Wo, 'bo': bo}
    _L1_gnn_all = _L1_gnn_setup()
    _L1_gnn_in = {k: v for k, v in _L1_gnn_all.items() if k in ('Wq', 'bq', 'Wk', 'bk', 'Wv', 'bv', 'Wo', 'bo')}
    del _L1_gnn_all

    def _L2_gnn_setup():
        import jax, jax.numpy as jnp
        import numpy as np
        ALPHA = 0.2
        key = jax.random.key(seed)
        k0, k1, k2, k3 = jax.random.split(key, 4)
        B, N, C, F = (64, 512, 256, 256)
        x = jax.random.normal(k0, (B, N, C), dtype=jnp.float32)
        W = jax.random.normal(k1, (C, F), dtype=jnp.float32) * (1.414 / np.sqrt(C + F))
        a = jax.random.normal(k2, (2 * F, 1), dtype=jnp.float32) * (1.414 / np.sqrt(2 * F + 1))
        beta = jnp.ones((1,), dtype=jnp.float32)
        mask = (jax.random.uniform(k3, (N, N)) < 0.3).astype(jnp.float32)
        return {'x': x, 'W': W, 'a': a, 'beta': beta, 'mask': mask}
    _L2_gnn_all = _L2_gnn_setup()
    _L2_gnn_in = {k: v for k, v in _L2_gnn_all.items() if k in ('W', 'a', 'beta')}
    del _L2_gnn_all

    def _L3_gnn_setup():
        import jax, jax.numpy as jnp
        import numpy as np
        key = jax.random.key(seed)
        k1, k2, k3, k4 = jax.random.split(key, 4)
        B, D, N = (4, 128, 256)
        scale = 1.0 / np.sqrt(2 * D)
        x = jax.random.normal(k1, (B, D, N), dtype=jnp.float32)
        W1 = jax.random.normal(k2, (D, D), dtype=jnp.float32) * scale
        W2 = jax.random.normal(k3, (D, D), dtype=jnp.float32) * scale
        b = jax.random.normal(k4, (D,), dtype=jnp.float32) * scale
        return {'x': x, 'W1': W1, 'W2': W2, 'b': b}
    _L3_gnn_all = _L3_gnn_setup()
    _L3_gnn_in = {k: v for k, v in _L3_gnn_all.items() if k in ('b',)}
    del _L3_gnn_all
    return {'x': x, 'adj': adj, 'L0_gnn_Wq': _L0_gnn_in['Wq'], 'L0_gnn_Wk': _L0_gnn_in['Wk'], 'L0_gnn_Wv': _L0_gnn_in['Wv'], 'L1_gnn_Wq': _L1_gnn_in['Wq'], 'L1_gnn_bq': _L1_gnn_in['bq'], 'L1_gnn_Wk': _L1_gnn_in['Wk'], 'L1_gnn_bk': _L1_gnn_in['bk'], 'L1_gnn_Wv': _L1_gnn_in['Wv'], 'L1_gnn_bv': _L1_gnn_in['bv'], 'L1_gnn_Wo': _L1_gnn_in['Wo'], 'L1_gnn_bo': _L1_gnn_in['bo'], 'L2_gnn_W': _L2_gnn_in['W'], 'L2_gnn_a': _L2_gnn_in['a'], 'L2_gnn_beta': _L2_gnn_in['beta'], 'L3_gnn_b': _L3_gnn_in['b']}

def reference(x, adj, L0_gnn_Wq, L0_gnn_Wk, L0_gnn_Wv, L1_gnn_Wq, L1_gnn_bq, L1_gnn_Wk, L1_gnn_bk, L1_gnn_Wv, L1_gnn_bv, L1_gnn_Wo, L1_gnn_bo, L2_gnn_W, L2_gnn_a, L2_gnn_beta, L3_gnn_b):
    import jax
    import jax.numpy as jnp

    def _L0_gnn_ref(neuron_states, adjacency, Wq, Wk, Wv):
        import jax, jax.numpy as jnp
        import numpy as np
        B, N, D = (8, 1024, 256)
        q = jnp.einsum('bnd,ed->bne', neuron_states, Wq)
        k = jnp.einsum('bnd,ed->bne', neuron_states, Wk)
        v = jnp.einsum('bnd,ed->bne', neuron_states, Wv)
        rel = jnp.einsum('bnd,bmd->bnm', q, k)
        rel = adjacency.T[None, :, :] * rel
        rel = rel / jnp.linalg.norm(rel, axis=2, keepdims=True)
        return jnp.einsum('bnm,bmd->bnd', rel, v)

    def _L1_gnn_ref(x, adj, Wq, bq, Wk, bk, Wv, bv, Wo, bo):
        import jax, jax.numpy as jnp
        import numpy as np
        B, N, D, H = (4, 1024, 256, 8)
        HD = D // H
        b, n, d = x.shape
        q = (x @ Wq + bq).reshape(b, n, H, HD)
        k = (x @ Wk + bk).reshape(b, n, H, HD)
        v = (x @ Wv + bv).reshape(b, n, H, HD)
        scores = jnp.einsum('bqhd,bkhd->bhqk', q, k) / jnp.sqrt(jnp.float32(HD))
        scores = scores + (1.0 - adj)[None, None, :, :] * -1000000000.0
        attn = jax.nn.softmax(scores, axis=-1)
        out = jnp.einsum('bhqk,bkhd->bqhd', attn, v).reshape(b, n, d)
        return out @ Wo + bo

    def _L2_gnn_ref(x, W, a, beta, mask):
        import jax, jax.numpy as jnp
        import numpy as np
        ALPHA = 0.2
        F_ = W.shape[1]
        h = jnp.einsum('bnc,cf->bnf', x, W)
        a1, a2 = (a[:F_, 0], a[F_:, 0])
        s1 = jnp.einsum('bnf,f->bn', h, a1)
        s2 = jnp.einsum('bnf,f->bn', h, a2)
        e = jax.nn.leaky_relu(s1[:, :, None] + s2[:, None, :], negative_slope=ALPHA)
        e = e * mask[None, :, :]
        att = jax.nn.softmax(e, axis=2)
        h_prime = jnp.einsum('bij,bjf->bif', att, h)
        return jax.nn.elu(h_prime + beta * h)

    def _L3_gnn_ref(x, W1, W2, b):
        import jax, jax.numpy as jnp
        import numpy as np
        A = jnp.einsum('od,bdn->bon', W1, x)
        C = jnp.einsum('od,bdn->bon', W2, x) + b[None, :, None]
        pre = A[:, :, None, :] + (C - A)[:, :, :, None]
        out = jnp.max(jax.nn.relu(pre), axis=-1)
        return out
    h = jnp.maximum(_layernorm(x, axis=-1), 0.0)
    x = x + _L0_gnn_ref(h, adj, L0_gnn_Wq, L0_gnn_Wk, L0_gnn_Wv)
    h = jnp.maximum(_layernorm(x, axis=-1), 0.0)
    x = x + _L1_gnn_ref(h, adj, L1_gnn_Wq, L1_gnn_bq, L1_gnn_Wk, L1_gnn_bk, L1_gnn_Wv, L1_gnn_bv, L1_gnn_Wo, L1_gnn_bo)
    h = jnp.maximum(_layernorm(x, axis=-1), 0.0)
    x = x + _L2_gnn_ref(h, L2_gnn_W, L2_gnn_a, L2_gnn_beta, adj)
    h = jnp.maximum(_layernorm(x, axis=-1), 0.0)
    x = x + _L3_gnn_ref(h, adj, adj, L3_gnn_b)
    return x

_drawn_inputs = setup_inputs


def setup_inputs(seed=0):
    import zlib

    import numpy as np

    out = dict(_drawn_inputs(seed))
    spreads = {'L1_gnn_bq': (0.0, 2.0),
     'L1_gnn_bk': (0.0, 2.0),
     'L1_gnn_bv': (0.0, 0.42),
     'L1_gnn_bo': (0.0, 0.314)}
    factors = {'L1_gnn_Wq': 7.862, 'L1_gnn_Wk': 4.811, 'L2_gnn_a': 8.0, 'L3_gnn_b': 58.919}
    for name, (base, spread) in spreads.items():
        noise = np.random.default_rng([zlib.crc32(name.encode()), seed]).standard_normal(out[name].shape)
        drawn = base * np.exp(spread * noise) if base else spread * noise
        out[name] = jnp.asarray(drawn.astype(out[name].dtype))
    for name, factor in factors.items():
        out[name] = (out[name] * factor).astype(out[name].dtype)
    return out
```

```python
from contextlib import ExitStack

import numpy as np

import concourse.bass as bass
from concourse import mybir
from concourse.alu_op_type import AluOpType as ALU

F32 = mybir.dt.float32
BF16 = mybir.dt.bfloat16
ACT = mybir.ActivationFunctionType
AX = mybir.AxisListType

B, N, D = 128, 128, 256
P = 128
GB = 4
NG = B // GB
C = D // P
COLS = GB * N
H, HD = 8, 32
HQ = P // HD
UNITS = C * GB
EPS = 1e-5
ALPHA = 0.2
MASK_UNIT, MASK_HI, MASK_LO = 125.0, 15616.0 * 512, 9.0 * 512

NORM0, LAYER0, LAYER1, TAIL1, LAYER2, LAYER3 = 0, 1, 2, 3, 3, 4
STEADY = range(LAYER3 + 2, NG)
ITERS = NG + LAYER3


class Group:

    def __init__(self, half, odd):
        self.half, self.odd = half, odd

    def ahead(self, n):
        return Group(self.half, self.odd + n)

    @property
    def parity(self):
        return self.odd % 2

    def times(self, k, plus=0):
        return self.half * (2 * k) + (self.odd * k + plus)

    def pair_times(self, k, plus=0):
        return self.half * k + ((self.odd // 2) * k + plus)

    def index(self):
        return self.half * 2 + self.odd

    def exists(self):
        return not isinstance(self.half, int) or 0 <= 2 * self.half + self.odd < NG


def wait(engine, semaphore, value):
    if isinstance(value, int) and value <= 0:
        return
    engine.wait_ge(semaphore, value)


class Counter:

    def __init__(self, semaphore, per_group):
        self.semaphore, self.per_group = semaphore, per_group

    def wait(self, engine, g, k):
        wait(engine, self.semaphore, g.times(self.per_group, k))


class Bank:

    def __init__(self, tensor, filled, drained, per_group):
        self.tensor = tensor
        self.filled, self.drained = Counter(filled, per_group), Counter(drained, per_group)


def build(nc, x, adj, w0q, w0k, w0v, w1q, b1q, w1k, b1k, w1v, b1v, w1o, b1o, w2, a2, beta2, b3, out):
    ctx = ExitStack()
    with ctx:
        def sb(name, shape, dt=F32):
            return ctx.enter_context(nc.sbuf_tensor(name, shape, dt))

        def sem(name):
            return ctx.enter_context(nc.semaphore(name))

        def counter(name, per_group):
            return Counter(sem(name), per_group)

        def bank(name, per_group):
            t = ctx.enter_context(nc.psum_tensor(name, [P, COLS], F32))
            return Bank(t, sem(name + "_filled"), sem(name + "_drained"), per_group)

        ident = sb("ident", [P, P])
        mask_eye = [sb(f"mask_eye{n}", [P, P], BF16) for n in range(2)]
        masked = sb("masked", [P, HQ, P], BF16)
        adj_sb = sb("adj_sb", [P, P])
        adj_T = sb("adj_T", [P, P])
        ones = sb("ones", [P, P])
        minus_half = sb("minus_half", [P, GB])
        head_rows = sb("head_rows", [P, HQ])
        A0 = sb("A0", [P, C, D])
        w0vT = sb("w0vT", [P, C, D])
        w0 = [sb(f"w0_{n}", [P, C, D]) for n in range(3)]
        w1q_sb, w1k_sb, w1v_sb, w1o_sb = (sb(n, [P, C, D]) for n in ("w1q", "w1k", "w1v", "w1o"))
        bq_cols, bk_cols, bv_cols = (sb(n, [P, C]) for n in ("bq_cols", "bk_cols", "bv_cols"))
        bq_scaled = sb("bq_scaled", [P, C])
        bv_wide = sb("bv_wide", [P, C, P])
        bo_rows = sb("bo_rows", [P, D])
        bias1 = sb("bias1", [P, D])
        w2_aug = sb("w2_aug", [P, C, D + 1])
        a_rows = sb("a_rows", [P, 2 * D])
        wa_junk = sb("wa_junk", [P, D])
        wa2 = sb("wa2", [P, C])
        wa2_wide = sb("wa2_wide", [P, C, P])
        beta_col = sb("beta_col", [P, 1])
        beta_eye = sb("beta_eye", [P, P])
        b3_col = sb("b3_col", [P, 1])

        x0 = [sb(f"x0_{p}", [P, GB, D]) for p in range(2)]
        x1 = [sb(f"x1_{p}", [P, GB, D]) for p in range(2)]
        x1_bias = [sb(f"x1_bias{p}", [P, GB, D]) for p in range(2)]
        x2 = [sb(f"x2_{p}", [P, GB, D]) for p in range(2)]
        x3 = [sb(f"x3_{p}", [P, GB, D]) for p in range(2)]
        x4 = [sb(f"x4_{p}", [P, GB, D]) for p in range(2)]
        h0 = [sb(f"h0_{p}", [P, GB, D]) for p in range(2)]
        xhat1 = sb("xhat1", [P, GB, D])
        xhat2 = sb("xhat2", [P, GB, D])
        h3 = sb("h3", [P, GB, D])
        stats = [sb(f"stats{n}", [P, GB, 6]) for n in range(4)]
        mv = [sb(f"mv{n}", [P, GB, 2]) for n in range(4)]
        veps = [sb(f"veps{n}", [P, GB]) for n in range(4)]
        negmean = [sb(f"negmean{n}", [P, GB]) for n in range(4)]
        rstd = [sb(f"rstd{n}", [P, GB]) for n in range(4)]
        shift = [sb(f"shift{n}", [P, GB]) for n in range(4)]
        hT0, hT1, hT2 = (sb(n, [P, C, COLS]) for n in ("hT0", "hT1", "hT2"))
        t0 = sb("t0", [P, C, COLS])
        relT = sb("relT", [P, COLS])
        relsq = sb("relsq", [P, COLS])
        normsq = sb("normsq", [P, GB])
        rnorm = sb("rnorm", [P, GB])
        GT = sb("GT", [P, C, COLS])
        qT = sb("qT", [P, C, COLS])
        kT = sb("kT", [P, C, COLS])
        k_wide = sb("k_wide", [P, C, GB, HQ, N])
        v1 = sb("v1", [P, GB, D])
        negmax = sb("negmax", [P, UNITS, HQ])
        probs = sb("probs", [P, 4, HQ, N])
        sums = sb("sums", [P, UNITS, HQ])
        rsums = sb("rsums", [P, UNITS, HQ])
        probsT = sb("probsT", [P, 2, HQ, N])
        attT1 = sb("attT1", [P, C, COLS])
        hp = sb("hp", [P, GB, D + 1])
        e_sum = sb("e_sum", [P, GB, N])
        e_leaky = sb("e_leaky", [P, GB, N])
        e_masked = sb("e_masked", [P, GB, N])
        max2, negmax2, sum2, rsum2 = (sb(n, [P, GB]) for n in ("max2", "negmax2", "sum2", "rsum2"))
        att2 = sb("att2", [P, GB, N])
        att2b = sb("att2b", [P, GB, N])
        att2T = sb("att2T", [P, GB, N])
        e_z = sb("e_z", [P, GB, D])
        x_relu = sb("x_relu", [P, GB, D])
        maxA = sb("maxA", [P, GB])
        gain3 = sb("gain3", [P, GB])
        gain3m = sb("gain3m", [P, GB])

        S = [bank(f"S{n}", UNITS // 2 + 1) for n in range(2)]
        PT = bank("PT", UNITS)
        PV = bank("PV", C)
        R1 = [bank(f"R1{n}", 4) for n in range(2)]
        R0 = bank("R0", 10)
        R2 = bank("R2", 12)

        weights_loaded = sem("weights_loaded")
        const_pool = sem("const_pool")
        const_dve = sem("const_dve")
        waits_taken = sem("waits_taken")
        const_pe = sem("const_pe")
        x0_loaded = [sem(f"x0_loaded{p}") for p in range(2)]
        stored = [sem(f"stored{p}") for p in range(2)]
        stats_done = [counter(f"stats_done{n}", GB) for n in range(4)]
        mv_done = [counter(f"mv_done{n}", GB) for n in range(4)]
        ln_small = [counter(f"ln_small{n}", 4 if n in (0, 3) else 3) for n in range(4)]
        h0_ready = counter("h0_ready", GB)
        xhat1_ready = counter("xhat1_ready", GB)
        xhat2_ready = counter("xhat2_ready", GB)
        h3_ready = counter("h3_ready", GB)
        relsq_ready = counter("relsq_ready", 1)
        rnorm_ready = counter("rnorm_ready", 1)
        x1_bias_ready = counter("x1_bias_ready", 1)
        k_wide_ready = counter("k_wide_ready", C)
        max_ready = counter("max_ready", UNITS)
        rsums_ready = counter("rsums_ready", UNITS)
        probs_ready = counter("probs_ready", UNITS)
        leaky_ready = counter("leaky_ready", 1)
        max2_ready = counter("max2_ready", 2)
        exp2_ready = counter("exp2_ready", 1)
        rsum2_ready = counter("rsum2_ready", 1)
        att2_ready = counter("att2_ready", 1)
        e_z_ready = counter("e_z_ready", 2)
        x3_ready = counter("x3_ready", 2)
        maxA_ready = counter("maxA_ready", 2)
        gain3_ready = counter("gain3_ready", 2)
        x4_ready = counter("x4_ready", GB)

        x_groups = x.rearrange("(g b) n d -> g n b d", b=GB)
        out_groups = out.rearrange("(g b) n d -> g n b d", b=GB)

        def rows(w):
            return w.rearrange("(c p) n -> p c n", p=P)

        def chunk_columns(tile, b):
            return [(tile[:, c:c + 1], b[c * P:(c + 1) * P].rearrange("(p o) -> p o", o=1)) for c in range(C)]

        def wide(b):
            return b.rearrange("(o n) -> o n", o=1).to_broadcast([P, b.shape[0]])

        WEIGHTS = [
            (adj_sb[:], adj), (w0[0][:], rows(w0q)), (w0[1][:], rows(w0k)), (w0[2][:], rows(w0v)),
            (w1q_sb[:], rows(w1q)), (w1k_sb[:], rows(w1k)), (w1v_sb[:], rows(w1v)), (w1o_sb[:], rows(w1o)),
            *chunk_columns(bq_cols, b1q), *chunk_columns(bk_cols, b1k), *chunk_columns(bv_cols, b1v),
            (bo_rows[:], wide(b1o)), (w2_aug[:, :, 0:D], rows(w2)),
            (a_rows[:], wide(a2.rearrange("f o -> (f o)"))), (beta_col[:], wide(beta2)),
            (b3_col[:], b3.rearrange("(p o) -> p o", o=1)),
        ]
        ALL_WEIGHTS = 16 * len(WEIGHTS)

        def apart(engine):
            engine.sem_inc(waits_taken, 1)

        def iterations(engine, iteration):
            for i in range(STEADY.start):
                iteration(Group(0, i))
            assert STEADY.start % 2 == 0 and len(STEADY) % 2 == 0
            with engine.Fori(STEADY.start // 2, STEADY.stop // 2) as half:
                iteration(Group(half, 0))
                iteration(Group(half, 1))
            for i in range(STEADY.stop, ITERS):
                iteration(Group(0, i))

        block = ctx.enter_context(nc.Block())

        @block.sync
        def _(sp):
            for dst, src in WEIGHTS:
                sp.dma_start(dst, src).then_inc(weights_loaded, 16)

            def load(g):
                R0.drained.wait(sp, g.ahead(-2), 10)
                sp.dma_start(x0[g.parity][:], x_groups[g.index()]).then_inc(x0_loaded[g.parity], 16)

            def store(g):
                x4_ready.wait(sp, g, GB)
                sp.dma_start(out_groups[g.index()], x4[g.parity][:]).then_inc(stored[g.parity], 16)

            load(Group(0, 0))

            def iteration(i):
                g = i.ahead(1 - NORM0)
                if g.exists():
                    load(g)
                g = i.ahead(-LAYER3)
                if g.exists():
                    store(g)

            for i in range(STEADY.start):
                iteration(Group(0, i))
            with sp.Fori(STEADY.start // 2, STEADY.stop // 2 - 1) as half:
                iteration(Group(half, 0))
                iteration(Group(half, 1))
            for i in range(STEADY.stop - 2, ITERS):
                iteration(Group(0, i))
            for p in range(2):
                sp.wait_ge(stored[p], 16 * (NG // 2))

        @block.tensor
        def _(pe):
            mm, transpose = nc.tensor.matmul, nc.tensor.transpose

            pe.wait_ge(weights_loaded, ALL_WEIGHTS)
            pe.wait_ge(const_pool, 2)
            for c in range(C):
                for k in range(C):
                    last = mm(R0.tensor[:, c * D:(c + 1) * D], w0[1][:, k, c * P:(c + 1) * P], w0[0][:, k, :],
                              start=(k == 0), stop=(k == C - 1))
            last.then_inc(const_pe, 1)
            for c in range(C):
                for k in range(C):
                    last = transpose(R2.tensor[:, c * D + k * P:c * D + (k + 1) * P],
                                     w0[2][:, k, c * P:(c + 1) * P], ident[:])
            last.then_inc(const_pe, 1)
            transpose(R1[0].tensor[:, 0:P], adj_sb[:], ident[:]).then_inc(const_pe, 1)
            pe.wait_ge(const_dve, CONST_BV)
            for c in range(C):
                last = mm(R1[1].tensor[:, 0:D], bv_wide[:, c, :], w1o_sb[:, c, :], start=(c == 0), stop=(c == C - 1))
            last.then_inc(const_pe, 1)
            pe.wait_ge(const_dve, CONST_DVE)
            pe.wait_ge(const_pool, CONST_POOL)

            def fill(bank, g, k):
                bank.drained.wait(pe, g, k)

            def done(last, bank):
                last.then_inc(bank.filled.semaphore, 1)

            def turn(bank, g, k, src, c):
                fill(bank, g, k)
                for b in range(GB):
                    last = transpose(bank.tensor[:, b * N:(b + 1) * N], src[:, b, c * P:(c + 1) * P], ident[:])
                done(last, bank)

            def project_T(bank, g, k, w, hT, m):
                fill(bank, g, k)
                for c in range(C):
                    last = mm(bank.tensor[:], w[:, c, m * P:(m + 1) * P], hT[:, c, :],
                              start=(c == 0), stop=(c == C - 1))
                done(last, bank)

            def project(bank, g, k, hT, w, half):
                fill(bank, g, k)
                for n, b in enumerate((2 * half, 2 * half + 1)):
                    for c in range(C):
                        last = mm(bank.tensor[:, n * D:(n + 1) * D], hT[:, c, b * N:(b + 1) * N], w[:, c, :],
                                  start=(c == 0), stop=(c == C - 1))
                done(last, bank)

            def layer0(g, step):
                if step < 2:
                    h0_ready.wait(pe, g, GB)
                    turn(R0, g, step, h0[g.parity], step)
                elif step < 4:
                    R0.drained.wait(pe, g, 2)
                    project_T(R0, g, step, A0, hT0, step - 2)
                elif step == 4:
                    fill(R0, g, 4)
                    for b in range(GB):
                        s = slice(b * N, (b + 1) * N)
                        for c in range(C):
                            last = mm(R0.tensor[:, s], t0[:, c, s], hT0[:, c, s], start=(c == 0), stop=(c == C - 1))
                    done(last, R0)
                elif step == 7:
                    fill(R0, g, 7)
                    relsq_ready.wait(pe, g, 1)
                    for b in range(GB):
                        s = slice(b * N, (b + 1) * N)
                        last = mm(R0.tensor[:, s], relsq[:, s], ones[:], start=True, stop=True)
                    done(last, R0)
                elif step < 7:
                    c = step - 5
                    fill(R0, g, step)
                    for b in range(GB):
                        s = slice(b * N, (b + 1) * N)
                        last = mm(R0.tensor[:, s], h0[g.parity][:, b, c * P:(c + 1) * P], relT[:, s],
                                  start=True, stop=True)
                    done(last, R0)
                else:
                    project(R0, g, step, GT, w0vT, step - 8)

            def turn1(g, c):
                xhat1_ready.wait(pe, g, GB)
                turn(R1[c], g, 0, xhat1, c)

            def both_hT1(g):
                for n in range(2):
                    R1[n].drained.wait(pe, g, 1)

            def keys(g, m):
                both_hT1(g)
                project_T(R1[m], g, 1, w1k_sb, hT1, m)

            def queries(g, m):
                project_T(R1[m], g, 2, w1q_sb, hT1, m)

            def values(g, half):
                project(R1[half], g, 3, hT1, w1v_sb, half)

            def scores(g, u):
                m, b = divmod(u, GB)
                bank = S[u % 2]
                fill(bank, g, u // 2)
                k_wide_ready.wait(pe, g, m + 1)
                R1[m].drained.wait(pe, g, 3)
                mm(bank.tensor[:], mask_eye[0][:], masked[:].rearrange("p h n -> p (h n)"), start=True, stop=False)
                mm(bank.tensor[:], mask_eye[1][:], masked[:].rearrange("p h n -> p (h n)"), start=False, stop=False)
                last = mm(bank.tensor[:], qT[:, m, b * N:(b + 1) * N],
                          k_wide[:, m, b, :, :].rearrange("p h n -> p (h n)"), start=False, stop=True)
                done(last, bank)

            def turn_probs(g, u):
                fill(PT, g, u)
                probs_ready.wait(pe, g, u + 1)
                for h in range(HQ):
                    last = transpose(PT.tensor[:, h * N:(h + 1) * N], probs[:, u % 4, h, :], ident[:])
                done(last, PT)

            def weigh_values(g, u):
                m, b = divmod(u, GB)
                if b == 0:
                    fill(PV, g, m)
                PT.drained.wait(pe, g, u + 1)
                if u == 0:
                    for n in range(2):
                        R1[n].drained.wait(pe, g, 4)
                for h in range(HQ):
                    last = mm(PV.tensor[h * HD:(h + 1) * HD, b * N:(b + 1) * N],
                              v1[:, b, m * P + h * HD:m * P + (h + 1) * HD], probsT[:, u % 2, h, :],
                              start=True, stop=True, tile_position=(0, h * HD))
                if b == GB - 1:
                    done(last, PV)

            def project_out(g, half):
                PV.drained.wait(pe, g, C)
                project(S[half], g, UNITS // 2, attT1, w1o_sb, half)

            def layer2(g, step):
                if step < 2:
                    xhat2_ready.wait(pe, g, GB)
                    turn(R2, g, step, xhat2, step)
                elif step == 6:
                    fill(R2, g, 6)
                    for c in range(C):
                        last = mm(R2.tensor[:], wa2_wide[:, c, :], hT2[:, c, :], start=(c == 0), stop=(c == C - 1))
                    done(last, R2)
                elif step < 6:
                    b = step - 2
                    fill(R2, g, step)
                    for c in range(C):
                        last = mm(R2.tensor[:, 0:D + 1], hT2[:, c, b * N:(b + 1) * N], w2_aug[:, c, :],
                                  start=(c == 0), stop=(c == C - 1))
                    done(last, R2)
                elif step == 7:
                    fill(R2, g, 7)
                    att2_ready.wait(pe, g, 1)
                    for b in range(GB):
                        last = transpose(R2.tensor[:, b * N:(b + 1) * N], att2b[:, b, :], ident[:])
                    done(last, R2)
                else:
                    fill(R2, g, step)
                    for n, b in enumerate((2 * (step - 8), 2 * (step - 8) + 1)):
                        last = mm(R2.tensor[:, n * D:(n + 1) * D], att2T[:, b, :], hp[:, b, 0:D], start=True, stop=True)
                    done(last, R2)

            def layer3(g, half):
                h3_ready.wait(pe, g, 2 * half + 2)
                fill(R2, g, 10 + half)
                last = mm(R2.tensor[:], adj_T[:],
                          h3[:, 2 * half:2 * half + 2, :].rearrange("p b d -> p (b d)"), start=True, stop=True)
                done(last, R2)

            def iteration(i):
                g0, g1, t1, g2, g3 = (i.ahead(-s) for s in (LAYER0, LAYER1, TAIL1, LAYER2, LAYER3))
                plan = [
                    (turn1, g1, 0), (turn1, g1, 1), (weigh_values, t1, 6), (layer0, g0, 0),
                    (keys, g1, 0), (turn_probs, t1, 7), (layer0, g0, 1), (keys, g1, 1),
                    (weigh_values, t1, 7), (layer0, g0, 2), (queries, g1, 0), (project_out, t1, 0),
                    (layer0, g0, 3), (project_out, t1, 1), (queries, g1, 1), (layer3, g3, 0),
                    (values, g1, 0), (layer0, g0, 4), (layer3, g3, 1), (values, g1, 1),
                    (scores, g1, 0), (layer0, g0, 5), (layer0, g0, 6),
                    (scores, g1, 1), (turn_probs, g1, 0), (layer0, g0, 7), (layer2, g2, 0), (layer2, g2, 1),
                    (scores, g1, 2), (layer2, g2, 2), (turn_probs, g1, 1), (layer2, g2, 3),
                    (weigh_values, g1, 0), (layer2, g2, 4),
                    (scores, g1, 3), (layer2, g2, 5), (turn_probs, g1, 2), (layer2, g2, 6),
                    (weigh_values, g1, 1), (layer0, g0, 8),
                    (scores, g1, 4), (turn_probs, g1, 3), (layer0, g0, 9), (weigh_values, g1, 2),
                    (scores, g1, 5), (layer2, g2, 7), (turn_probs, g1, 4), (layer2, g2, 8),
                    (weigh_values, g1, 3), (layer2, g2, 9),
                    (scores, g1, 6), (turn_probs, g1, 5), (weigh_values, g1, 4),
                    (scores, g1, 7), (turn_probs, g1, 6), (weigh_values, g1, 5),
                ]
                for step, g, n in plan:
                    if g.exists():
                        step(g, n)

            iterations(pe, iteration)

        @block.scalar
        def _(act):
            activation = nc.scalar.activation

            def copy_out(bank, g, k, dst, src=None, func=ACT.Copy, **kw):
                bank.filled.wait(act, g, k + 1)
                activation(dst, bank.tensor[:] if src is None else src, func, **kw)\
                    .then_inc(bank.drained.semaphore, 1)

            def norm0(g, _):
                ln_small[0].wait(act, g, 4)
                R0.filled.wait(act, g.ahead(-1), 0)
                for b in range(GB):
                    activation(h0[g.parity][:, b, :], x0[g.parity][:, b, :], ACT.Relu, bias=shift[0][:, b:b + 1],
                               scale=rstd[0][:, b:b + 1]).then_inc(h0_ready.semaphore, 1)

            def norm3(g, _):
                ln_small[3].wait(act, g, 4)
                R2.filled.wait(act, g, 0)
                for b in range(GB):
                    activation(h3[:, b, :], x3[g.parity][:, b, :], ACT.Relu, bias=shift[3][:, b:b + 1],
                               scale=rstd[3][:, b:b + 1]).then_inc(h3_ready.semaphore, 1)

            def layer0(g, k):
                if k == 1:
                    copy_out(R0, g, 1, hT0[:, 1, :])
                elif k == 3:
                    copy_out(R0, g, 3, t0[:, 1, :])
                elif k == 6:
                    copy_out(R0, g, 6, GT[:, 1, :])

            def relu_hT1(g, c):
                copy_out(R1[c], g, 0, hT1[:, c, :], func=ACT.Relu)

            def queries(g, m):
                copy_out(R1[m], g, 2, qT[:, m, :], func=ACT.Identity, bias=bq_scaled[:, m:m + 1], scale=HD ** -0.5)

            def values(g, half):
                copy_out(R1[half], g, 3, v1[:, 2 * half:2 * half + 2, :].rearrange("p b d -> p (b d)"))

            def exps(g, u):
                bank = S[u % 2]
                max_ready.wait(act, g, u + 1)
                for h in range(HQ):
                    last = activation(probs[:, u % 4, h, :], bank.tensor[:, h * N:(h + 1) * N], ACT.Exp,
                                      bias=negmax[:, u, h:h + 1], accum_out=sums[:, u, h:h + 1])
                last.then_inc(bank.drained.semaphore, 1)

            def probs_out(g, u):
                copy_out(PT, g, u, probsT[:, u % 2, :, :].rearrange("p h n -> p (h n)"))

            def attention_out(g, m):
                copy_out(PV, g, m, attT1[:, m, :])

            def layer2(g, k):
                if k == 0:
                    copy_out(R2, g, 0, hT2[:, 0, :], func=ACT.Relu)
                elif k < 6:
                    copy_out(R2, g, k, hp[:, k - 2, :], src=R2.tensor[:, 0:D + 1])
                elif k == 6:
                    R2.filled.wait(act, g, 7)
                    R2.drained.wait(act, g, 6)
                    for b in range(GB):
                        last = activation(e_sum[:, b, :], R2.tensor[:, b * N:(b + 1) * N], ACT.Identity,
                                          bias=hp[:, b, D:D + 1])
                    last.then_inc(R2.drained.semaphore, 1)
                elif k == 7:
                    copy_out(R2, g, 7, att2T[:].rearrange("p b n -> p (b n)"))
                else:
                    half = k - 8
                    R2.filled.wait(act, g, k + 1)
                    activation(e_z[:, 2 * half:2 * half + 2, :].rearrange("p b d -> p (b d)"), R2.tensor[:], ACT.Exp)\
                        .then_inc(e_z_ready.semaphore, 1)

            def softmax2(g, _):
                max2_ready.wait(act, g, 2)
                for b in range(GB):
                    last = activation(att2[:, b, :], e_masked[:, b, :], ACT.Exp, bias=negmax2[:, b:b + 1],
                                      accum_out=sum2[:, b:b + 1])
                last.then_inc(exp2_ready.semaphore, 1)

            act.wait_ge(const_dve, CONST_DVE)

            def iteration(i):
                n0, g0, g1, t1, g2 = (i.ahead(-s) for s in (NORM0, LAYER0, LAYER1, TAIL1, LAYER2))
                plan = [
                    (relu_hT1, g1, 0), (layer0, g0, 1), (queries, g1, 0), (layer0, g0, 3), (queries, g1, 1),
                    (values, g1, 0), (exps, g1, 0), (layer0, g0, 6), (exps, g1, 1), (probs_out, g1, 0),
                    (layer2, g2, 0), (exps, g1, 2), (layer2, g2, 2), (layer2, g2, 3), (layer2, g2, 4),
                    (exps, g1, 3), (layer2, g2, 5), (probs_out, g1, 2), (layer2, g2, 6),
                    (exps, g1, 4), (softmax2, g2, 0), (exps, g1, 5), (layer2, g2, 7), (probs_out, g1, 4),
                    (layer2, g2, 8), (attention_out, g1, 0), (layer2, g2, 9), (norm0, n0, 0),
                    (exps, g1, 6), (exps, g1, 7), (probs_out, g1, 6), (norm3, g2, 0),
                ]
                for step, g, n in plan:
                    if g.exists():
                        step(g, n)

            iterations(act, iteration)

        @block.vector
        def _(dve):
            v = nc.vector
            built = [0]

            def constant(instruction):
                instruction.then_inc(const_dve, 1)
                built[0] += 1
                dve.wait_ge(const_dve, built[0])

            dve.wait_ge(weights_loaded, ALL_WEIGHTS)
            dve.wait_ge(const_pool, 3)
            for c in range(C):
                constant(v.tensor_scalar(bv_wide[:, c, :], ones[:], bv_cols[:, c:c + 1], None, ALU.mult))
            assert built[0] == CONST_BV
            for n, part in enumerate((MASK_HI, MASK_LO)):
                constant(v.tensor_scalar(mask_eye[n][:], ident[:], -part, None, ALU.mult))
            for h in range(HQ):
                constant(v.tensor_scalar(masked[:, h, :], adj_sb[:], -MASK_UNIT, MASK_UNIT, ALU.mult, ALU.add))
            constant(v.tensor_scalar(bq_scaled[:], bq_cols[:], HD ** -0.5, None, ALU.mult))
            for c in range(C):
                for half, col in enumerate((w2_aug[:, c, D:D + 1], wa2[:, c:c + 1])):
                    constant(v.tensor_tensor_reduce(wa_junk[:], w2_aug[:, c, 0:D], a_rows[:, half * D:(half + 1) * D],
                                                    1.0, 0.0, ALU.mult, ALU.add, col))
                constant(v.tensor_scalar(wa2_wide[:, c, :], ones[:], wa2[:, c:c + 1], None, ALU.mult))
            constant(v.tensor_scalar(beta_eye[:], ident[:], beta_col[:, 0:1], None, ALU.mult))
            dve.wait_ge(const_pe, 1)
            constant(v.tensor_copy(A0[:].rearrange("p c d -> p (c d)"), R0.tensor[:]))
            dve.wait_ge(const_pe, 2)
            constant(v.tensor_copy(w0vT[:].rearrange("p c d -> p (c d)"), R2.tensor[:]))
            dve.wait_ge(const_pe, 3)
            constant(v.tensor_copy(adj_T[:], R1[0].tensor[:, 0:P]))
            dve.wait_ge(const_pe, 4)
            constant(v.tensor_tensor(bias1[:], R1[1].tensor[:, 0:D], bo_rows[:], ALU.add))
            assert built[0] == CONST_DVE

            def copy_out(bank, g, k, dst):
                bank.filled.wait(dve, g, k + 1)
                v.tensor_copy(dst, bank.tensor[:]).then_inc(bank.drained.semaphore, 1)

            def relu_out(bank, g, k, dst):
                bank.filled.wait(dve, g, k + 1)
                v.tensor_scalar(dst, bank.tensor[:], 0.0, None, ALU.max).then_inc(bank.drained.semaphore, 1)

            def statistics(n, g, src, batches, last):
                for b in batches:
                    v.bn_stats(stats[n][:, b, :], src[:, b, :]).then_inc(stats_done[n].semaphore, 1)
                if last:
                    ln_small[n].wait(dve, g, 0)
                    for b in range(GB):
                        stats_done[n].wait(dve, g, b + 1)
                        apart(dve)
                        v.bn_aggr(mv[n][:, b, :], stats[n][:, b, :]).then_inc(mv_done[n].semaphore, 1)

            def norm0(g, _):
                dve.wait_ge(x0_loaded[g.parity], g.pair_times(16, 16))
                statistics(0, g, x0[g.parity], range(GB), True)

            def layer0(g, k):
                if k == 0:
                    copy_out(R0, g, 0, hT0[:, 0, :])
                elif k == 2:
                    copy_out(R0, g, 2, t0[:, 0, :])
                elif k == 4:
                    R0.filled.wait(dve, g, 5)
                    v.tensor_tensor(relT[:].rearrange("p (b n) -> p b n", b=GB),
                                    R0.tensor[:].rearrange("p (b n) -> p b n", b=GB),
                                    adj_sb[:].unsqueeze(1).to_broadcast([P, GB, N]), ALU.mult)\
                        .then_inc(R0.drained.semaphore, 1)
                elif k == 5:
                    copy_out(R0, g, 5, GT[:, 0, :])
                elif k == 7:
                    R0.filled.wait(dve, g, 8)
                    rnorm_ready.wait(dve, g, 0)
                    v.tensor_copy(normsq[:], R0.tensor[:, 0:COLS:N]).then_inc(R0.drained.semaphore, 1)
                else:
                    half = k - 8
                    R0.filled.wait(dve, g, k + 1)
                    if half == 0:
                        rnorm_ready.wait(dve, g, 1)
                        xhat1_ready.wait(dve, g, 0)
                        x1_bias_ready.wait(dve, g, 0)
                    for n, b in enumerate((2 * half, 2 * half + 1)):
                        last = v.scalar_tensor_tensor(x1[g.parity][:, b, :], R0.tensor[:, n * D:(n + 1) * D],
                                                      rnorm[:, b:b + 1], x0[g.parity][:, b, :], ALU.mult, ALU.add)
                    last.then_inc(R0.drained.semaphore, 1)

            def norm1(g, _):
                R0.drained.wait(dve, g, 10)
                statistics(1, g, x1[g.parity], range(GB), True)

            def relu_hT1(g, c):
                relu_out(R1[c], g, 0, hT1[:, c, :])

            def keys(g, m):
                R1[m].filled.wait(dve, g, 2)
                k_wide_ready.wait(dve, g, 0)
                v.tensor_scalar(kT[:, m, :], R1[m].tensor[:], bk_cols[:, m:m + 1], None, ALU.add)\
                    .then_inc(R1[m].drained.semaphore, 1)

            def values(g, half):
                copy_out(R1[half], g, 3, v1[:, 2 * half:2 * half + 2, :].rearrange("p b d -> p (b d)"))

            def maxima(g, u):
                bank = S[u % 2]
                bank.filled.wait(dve, g.ahead(0), u // 2 + 1)
                v.tensor_reduce(negmax[:, u, :], bank.tensor[:].rearrange("p (h n) -> p h n", h=HQ), AX.X,
                                ALU.max, negate=True).then_inc(max_ready.semaphore, 1)

            def invert_sums(g, u):
                S[u % 2].drained.wait(dve, g, u // 2 + 1)
                probs_ready.wait(dve, g.ahead(-1), u + 1)
                v.reciprocal(rsums[:, u, :], sums[:, u, :]).then_inc(rsums_ready.semaphore, 1)

            def probs_out(g, u):
                copy_out(PT, g, u, probsT[:, u % 2, :, :].rearrange("p h n -> p (h n)"))

            def attention_out(g, m):
                copy_out(PV, g, m, attT1[:, m, :])

            def residual1(g, half):
                bank = S[half]
                bank.filled.wait(dve, g, UNITS // 2 + 1)
                x1_bias_ready.wait(dve, g, 1)
                if half == 0:
                    xhat2_ready.wait(dve, g, 0)
                rows_ = slice(2 * half, 2 * half + 2)
                last = v.tensor_tensor(x2[g.parity][:, rows_, :].rearrange("p b d -> p (b d)"), bank.tensor[:],
                                       x1_bias[g.parity][:, rows_, :].rearrange("p b d -> p (b d)"), ALU.add)
                last.then_inc(bank.drained.semaphore, 1)
                bank.drained.wait(dve, g, UNITS // 2 + 1)
                statistics(2, g, x2[g.parity], (2 * half, 2 * half + 1), half == 1)

            def layer2(g, k):
                if k == 1:
                    relu_out(R2, g, 1, hT2[:, 1, :])
                elif k == 7:
                    R2.drained.wait(dve, g, 7)
                    v.scalar_tensor_tensor(e_leaky[:], e_sum[:], ALPHA, e_sum[:], ALU.mult, ALU.max)\
                        .then_inc(leaky_ready.semaphore, 1)
                    leaky_ready.wait(dve, g, 1)
                    exp2_ready.wait(dve, g, 0)
                    apart(dve)
                    for b in range(GB):
                        last = v.tensor_tensor_reduce(e_masked[:, b, :], e_leaky[:, b, :], adj_sb[:], 1.0, -3.4e38,
                                                      ALU.mult, ALU.max, max2[:, b:b + 1])
                    last.then_inc(max2_ready.semaphore, 1)
                    max2_ready.wait(dve, g, 1)
                    v.tensor_scalar(negmax2[:], max2[:], -1.0, None, ALU.mult).then_inc(max2_ready.semaphore, 1)

            def weights2(g, _):
                exp2_ready.wait(dve, g, 1)
                v.reciprocal(rsum2[:], sum2[:]).then_inc(rsum2_ready.semaphore, 1)
                rsum2_ready.wait(dve, g, 1)
                for b in range(GB):
                    last = v.scalar_tensor_tensor(att2b[:, b, :], att2[:, b, :], rsum2[:, b:b + 1], beta_eye[:],
                                                  ALU.mult, ALU.add)
                last.then_inc(att2_ready.semaphore, 1)

            def elu(g, half):
                rows_ = slice(2 * half, 2 * half + 2)
                flat = lambda t: t[:, rows_, :].rearrange("p b d -> p (b d)")
                e_z_ready.wait(dve, g, half + 1)
                last = v.scalar_tensor_tensor(flat(x_relu), R2.tensor[:], 0.0, flat(x2[g.parity]), ALU.max, ALU.add)
                last.then_inc(R2.drained.semaphore, 1)
                R2.drained.wait(dve, g, 9 + half)
                if half == 0:
                    x4_ready.wait(dve, g.ahead(-1), 0)
                v.scalar_tensor_tensor(flat(x3[g.parity]), flat(e_z), 1.0, flat(x_relu), ALU.min, ALU.add)\
                    .then_inc(x3_ready.semaphore, 1)
                x3_ready.wait(dve, g, half + 1)
                statistics(3, g, x3[g.parity], (2 * half, 2 * half + 1), half == 1)

            def layer3(g, half):
                R2.filled.wait(dve, g, 11 + half)
                v.tensor_reduce(maxA[:, 2 * half:2 * half + 2], R2.tensor[:].rearrange("p (b n) -> p b n", b=2),
                                AX.X, ALU.max).then_inc(R2.drained.semaphore, 1)
                if half == 1:
                    R2.drained.wait(dve, g, 12)
                    v.tensor_scalar(gain3[:], maxA[:], b3_col[:, 0:1], 0.0, ALU.add, ALU.max)\
                        .then_inc(gain3_ready.semaphore, 1)
                    gain3_ready.wait(dve, g, 1)
                    x4_ready.wait(dve, g, 0)
                    v.tensor_scalar(gain3m[:], gain3[:], -1.0, None, ALU.add).then_inc(gain3_ready.semaphore, 1)

            def iteration(i):
                n0, g0, g1, t1, g2, g3 = (i.ahead(-s) for s in (NORM0, LAYER0, LAYER1, TAIL1, LAYER2, LAYER3))
                plan = [
                    (relu_hT1, g1, 1), (layer0, g0, 0), (keys, g1, 0), (probs_out, t1, 7), (keys, g1, 1),
                    (attention_out, t1, 1), (layer0, g0, 2), (residual1, t1, 0), (residual1, t1, 1),
                    (layer3, g3, 0), (layer0, g0, 4), (layer3, g3, 1), (values, g1, 1),
                    (maxima, g1, 0), (layer0, g0, 5), (invert_sums, g1, 0), (maxima, g1, 1), (layer0, g0, 7),
                    (invert_sums, g1, 1), (layer2, g2, 1), (maxima, g1, 2), (probs_out, g1, 1),
                    (invert_sums, g1, 2), (maxima, g1, 3), (layer0, g0, 8), (layer2, g2, 7), (invert_sums, g1, 3),
                    (maxima, g1, 4), (probs_out, g1, 3), (layer0, g0, 9), (weights2, g2, 0), (invert_sums, g1, 4),
                    (maxima, g1, 5), (norm1, g0, 0), (invert_sums, g1, 5), (norm0, n0, 0), (elu, g2, 0),
                    (maxima, g1, 6), (probs_out, g1, 5), (elu, g2, 1), (invert_sums, g1, 6),
                    (maxima, g1, 7), (invert_sums, g1, 7),
                ]
                for step, g, n in plan:
                    if g.exists():
                        step(g, n)

            iterations(dve, iteration)

        @block.gpsimd
        def _(pool):
            p = nc.gpsimd
            p.memset(ident[:], 0.0).then_inc(const_pool, 1)
            pool.wait_ge(const_pool, 1)
            p.affine_select(out=ident[:], in_=ident[:], compare_op=ALU.not_equal, fill=1.0, base=0,
                            pattern=[[-1, P]], channel_multiplier=1).then_inc(const_pool, 1)
            p.memset(ones[:], 1.0).then_inc(const_pool, 1)
            p.memset(minus_half[:], -0.5).then_inc(const_pool, 1)
            p.memset(head_rows[:], 1.0).then_inc(const_pool, 1)
            for base, sign in ((0, 1), (HD - 1, -1)):
                pool.wait_ge(const_pool, 5 if sign > 0 else 6)
                p.affine_select(out=head_rows[:], in_=head_rows[:], compare_op=ALU.is_ge, fill=0.0, base=base,
                                pattern=[[-sign * HD, HQ]], channel_multiplier=sign).then_inc(const_pool, 1)
            pool.wait_ge(const_pool, CONST_POOL)
            pool.wait_ge(const_dve, CONST_DVE)

            def small(n, g):
                mv_done[n].wait(pool, g, GB)
                apart(pool)
                p.tensor_scalar(veps[n][:], mv[n][:, :, 1], EPS, 1.0, ALU.add, ALU.mult)\
                    .then_inc(ln_small[n].semaphore, 1)
                p.tensor_scalar(negmean[n][:], mv[n][:, :, 0], -1.0, 0.0, ALU.mult, ALU.add)\
                    .then_inc(ln_small[n].semaphore, 1)
                ln_small[n].wait(pool, g, 1)
                if n == 0:
                    h0_ready.wait(pool, g, 0)
                if n == 3:
                    h3_ready.wait(pool, g, 0)
                p.tensor_tensor(rstd[n][:], veps[n][:], minus_half[:], ALU.pow).then_inc(ln_small[n].semaphore, 1)
                ln_small[n].wait(pool, g, 3)
                if n in (0, 3):
                    p.tensor_tensor(shift[n][:], negmean[n][:], rstd[n][:], ALU.mult).then_inc(ln_small[n].semaphore, 1)

            def normalise(n, g, dst, src, ready):
                small(n, g)
                apart(pool)
                for b in range(GB):
                    p.tensor_scalar(dst[:, b, :], src[:, b, :], negmean[n][:, b:b + 1], rstd[n][:, b:b + 1],
                                    ALU.add, ALU.mult).then_inc(ready.semaphore, 1)

            def norm0(g, _):
                small(0, g)

            def norm1(g, _):
                R1[1].filled.wait(pool, g, 0)
                normalise(1, g, xhat1, x1[g.parity], xhat1_ready)

            def norm2(g, _):
                R2.filled.wait(pool, g, 0)
                normalise(2, g, xhat2, x2[g.parity], xhat2_ready)

            def norm3(g, _):
                small(3, g)

            def bias(g, _):
                S[1].drained.wait(pool, g.ahead(-1), 0)
                R0.drained.wait(pool, g, 10)
                p.tensor_tensor(x1_bias[g.parity][:], x1[g.parity][:],
                                bias1[:].unsqueeze(1).to_broadcast([P, GB, D]), ALU.add)\
                    .then_inc(x1_bias_ready.semaphore, 1)

            def squares(g, _):
                R0.drained.wait(pool, g, 5)
                p.tensor_tensor(relsq[:], relT[:], relT[:], ALU.mult).then_inc(relsq_ready.semaphore, 1)

            def invert_norm(g, _):
                R0.drained.wait(pool, g, 8)
                p.tensor_tensor(rnorm[:], normsq[:], minus_half[:], ALU.pow).then_inc(rnorm_ready.semaphore, 1)

            def widen_keys(g, m):
                R1[m].drained.wait(pool, g, 2)
                apart(pool)
                for h in range(HQ):
                    last = p.tensor_scalar(k_wide[:, m, :, h, :], kT[:, m, :].rearrange("p (b n) -> p b n", b=GB),
                                           head_rows[:, h:h + 1], 0.0, ALU.mult, ALU.add)
                last.then_inc(k_wide_ready.semaphore, 1)

            def normalise_probs(g, u):
                rsums_ready.wait(pool, g, u + 1)
                p.tensor_tensor(probs[:, u % 4, :, :], probs[:, u % 4, :, :],
                                rsums[:, u, :].unsqueeze(2).to_broadcast([P, HQ, N]), ALU.mult)\
                    .then_inc(probs_ready.semaphore, 1)

            def residual3(g, _):
                gain3_ready.wait(pool, g, 2)
                wait(pool, stored[g.parity], g.pair_times(16))
                apart(pool)
                for b in range(GB):
                    p.tensor_scalar(x4[g.parity][:, b, :], x3[g.parity][:, b, :], 1.0, gain3m[:, b:b + 1],
                                    ALU.mult, ALU.add).then_inc(x4_ready.semaphore, 1)

            def iteration(i):
                n0, g0, g1, g2, g3 = (i.ahead(-s) for s in (NORM0, LAYER0, LAYER1, LAYER2, LAYER3))
                plan = [
                    (widen_keys, g1, 0), (widen_keys, g1, 1), (norm2, g2, 0), (squares, g0, 0),
                    (normalise_probs, g1, 0), (residual3, g3, 0), (invert_norm, g0, 0), (normalise_probs, g1, 1),
                    (normalise_probs, g1, 2), (normalise_probs, g1, 3), (normalise_probs, g1, 4),
                    (norm1, g0, 0), (normalise_probs, g1, 5), (norm0, n0, 0),
                    (normalise_probs, g1, 6), (norm3, g2, 0), (normalise_probs, g1, 7), (bias, g0, 0),
                ]
                for step, g, n in plan:
                    if g.exists():
                        step(g, n)

            iterations(pool, iteration)


CONST_BV, CONST_DVE, CONST_POOL = C, 20, 7

_INS = ["x", "adj", "L0_gnn_Wq", "L0_gnn_Wk", "L0_gnn_Wv", "L1_gnn_Wq", "L1_gnn_bq", "L1_gnn_Wk", "L1_gnn_bk",
        "L1_gnn_Wv", "L1_gnn_bv", "L1_gnn_Wo", "L1_gnn_bo", "L2_gnn_W", "L2_gnn_a", "L2_gnn_beta", "L3_gnn_b"]


def kernel(**inputs):
    import concourse.bacc as bacc
    from concourse.bass_utils import run_bass_kernel_spmd

    nc = bacc.Bacc("TRN2", target_bir_lowering=False, num_devices=1)
    arrays, args = {}, []
    for name in _INS:
        a = np.ascontiguousarray(inputs[name])
        arrays[f"in_{name}"] = a
        args.append(nc.dram_tensor(f"in_{name}", a.shape, mybir.dt.from_np(a.dtype), kind="ExternalInput").ap())
    args.append(nc.dram_tensor("out", (B, N, D), F32, kind="ExternalOutput").ap())
    build(nc, *args)
    r = run_bass_kernel_spmd(nc, [arrays], core_ids=[0])
    return r.results[0]["out"]
```

```python
from contextlib import ExitStack

import numpy as np

import concourse.bass as bass
from concourse import mybir
from concourse.alu_op_type import AluOpType as ALU

F32, F16 = mybir.dt.float32, mybir.dt.float16
ACT = mybir.ActivationFunctionType
AX = mybir.AxisListType

B, N, D = 128, 128, 256
P = 128
GB = 4
NG = B // GB
C = D // P
COLS = GB * N
H, HD = 8, 32
HQ = P // HD
UNITS = C * GB
EPS = 1e-5
ALPHA = 0.2
BIG = 3.4e38
PASSES = ((0, 0), (0, 1), (1, 0))

NORM0, LAYER0, PROJ1, ATTN1, LAYER2, LAYER3 = 0, 1, 2, 3, 4, 5
STEADY = range(LAYER3 + 1, NG)
ITERS = NG + LAYER3


class Group:

    def __init__(self, half, odd):
        self.half, self.odd = half, odd

    def ahead(self, n):
        return Group(self.half, self.odd + n)

    @property
    def parity(self):
        return self.odd % 2

    def times(self, k, plus=0):
        return self.half * (2 * k) + (self.odd * k + plus)

    def pair_times(self, k, plus=0):
        return self.half * k + ((self.odd // 2) * k + plus)

    def index(self):
        return self.half * 2 + self.odd

    def exists(self):
        return not isinstance(self.half, int) or 0 <= 2 * self.half + self.odd < NG


def counts(value):
    return not isinstance(value, int) or value > 0


class Counter:

    def __init__(self, semaphore, per_group):
        self.sem, self.per_group = semaphore, per_group

    def at(self, g, k):
        return g.times(self.per_group, k)


class Bank:

    def __init__(self, tensor, filled, drained, per_group):
        self.tensor = tensor
        self.filled, self.drained = Counter(filled, per_group), Counter(drained, per_group)


def build(nc, x, adj, w0q, w0k, w0v, w1q, b1q, w1k, b1k, w1v, b1v, w1o, b1o, w2, a2, beta2, b3, out):
    ctx = ExitStack()
    with ctx:
        def sb(name, shape, dt=F32):
            return ctx.enter_context(nc.sbuf_tensor(name, shape, dt))

        def pair(name, shape):
            return [sb(f"{name}_{part}", shape, F16) for part in ("high", "low")]

        def sem(name):
            return ctx.enter_context(nc.semaphore(name))

        def counter(name, per_group):
            return Counter(sem(name), per_group)

        def bank(name, per_group):
            t = ctx.enter_context(nc.psum_tensor(name, [P, COLS], F32))
            return Bank(t, sem(name + "_filled"), sem(name + "_drained"), per_group)

        ident = sb("ident", [P, P])
        mask1 = sb("mask1", [P, P])
        adj_sb = sb("adj_sb", [P, P])
        adj_T = sb("adj_T", [P, P])
        ones = sb("ones", [P, P])
        minus_half = sb("minus_half", [P, GB])
        head_rows = sb("head_rows", [P, HQ])
        A0 = pair("A0", [P, C, D])
        w0vT = pair("w0vT", [P, C, D])
        w1q_sb, w1k_sb, w1v_sb, w1o_sb = (pair(n, [P, C, D]) for n in ("w1q", "w1k", "w1v", "w1o"))
        bq_cols, bk_cols, bv_cols = (sb(n, [P, C]) for n in ("bq_cols", "bk_cols", "bv_cols"))
        bq_scaled = sb("bq_scaled", [P, C])
        bias1 = sb("bias1", [P, D])
        w2_aug = pair("w2_aug", [P, C, D + 1])
        wa2 = sb("wa2", [P, C])
        wa2_wide = pair("wa2_wide", [P, C, P])
        beta_col = sb("beta_col", [P, 1])
        beta_eye = sb("beta_eye", [P, P])
        b3_col = sb("b3_col", [P, 1])

        x0 = [sb(f"x0_{p}", [P, GB, D]) for p in range(2)]
        x1 = [sb(f"x1_{p}", [P, GB, D]) for p in range(2)]
        x1_bias = [sb(f"x1_bias{p}", [P, GB, D]) for p in range(2)]
        x2 = [sb(f"x2_{p}", [P, GB, D]) for p in range(2)]
        x3 = [sb(f"x3_{p}", [P, GB, D]) for p in range(2)]
        xhat0 = sb("xhat0", [P, GB, D])
        xhat1 = sb("xhat1", [P, GB, D])
        xhat2 = sb("xhat2", [P, GB, D])
        h3 = sb("h3", [P, GB, D])
        stats = [sb(f"stats{n}", [P, GB, 6]) for n in range(4)]
        mv = [sb(f"mv{n}", [P, GB, 2]) for n in range(4)]
        veps = [sb(f"veps{n}", [P, GB]) for n in range(4)]
        negmean = [sb(f"negmean{n}", [P, GB]) for n in range(4)]
        rstd = [sb(f"rstd{n}", [P, GB]) for n in range(4)]
        shift = [sb(f"shift{n}", [P, GB]) for n in range(4)]
        hT0 = sb("hT0", [P, C, COLS])
        hT0_parts, hT1, hT2 = (pair(n, [P, C, COLS]) for n in ("hT0_parts", "hT1", "hT2"))
        t0 = sb("t0", [P, C, COLS])
        relT = sb("relT", [P, COLS])
        relsq = sb("relsq", [P, COLS])
        normsq = sb("normsq", [P, GB])
        rnorm = sb("rnorm", [P, GB])
        v0 = sb("v0", [P, GB, D])
        qT = [sb(f"qT{p}", [P, C, COLS]) for p in range(2)]
        kT = sb("kT", [P, C, COLS])
        k_wide = [sb(f"k_wide{p}", [P, C, GB, HQ, N]) for p in range(2)]
        v1 = [sb(f"v1_{p}", [P, GB, D]) for p in range(2)]
        scores1 = sb("scores1", [P, 2, HQ, N])
        negmax = sb("negmax", [P, UNITS, HQ])
        probs = sb("probs", [P, 4, HQ, N])
        sums = sb("sums", [P, UNITS, HQ])
        rsums = sb("rsums", [P, UNITS, HQ])
        probsT = sb("probsT", [P, 2, HQ, N])
        attT1 = pair("attT1", [P, C, COLS])
        hp = sb("hp", [P, GB, D + 1])
        e_sum = sb("e_sum", [P, GB, N])
        e_leaky = sb("e_leaky", [P, GB, N])
        e_masked = sb("e_masked", [P, GB, N])
        max2, negmax2, sum2, rsum2 = (sb(n, [P, GB]) for n in ("max2", "negmax2", "sum2", "rsum2"))
        att2 = sb("att2", [P, GB, N])
        att2b = sb("att2b", [P, GB, N])
        att2T = sb("att2T", [P, GB, N])
        e_z = sb("e_z", [P, GB, D])
        maxA = sb("maxA", [P, GB])
        gain3 = sb("gain3", [P, GB])
        gain3m = sb("gain3m", [P, GB])

        def staged(parity, at, shape):
            flat = k_wide[parity][:].rearrange("p c b h n -> p (c b h n)")[:, at:at + int(np.prod(shape))]
            return flat.rearrange("p (c d) -> p c d", c=shape[0]) if len(shape) == 2 else flat

        w0q_in, w0k_in, w0v_in, w1q_in, w1k_in, w1v_in, w1o_in = (staged(1, n * C * D, [C, D]) for n in range(7))
        w2_in = staged(0, 0, [C, D + 1])
        at = C * (D + 1)
        a_rows, wa_junk, one_minus_adj, bo_rows = (staged(0, at + k * D, [n * D]) for k, n in
                                                   ((0, 2), (2, 1), (3, 1), (4, 1)))
        wa2_in, bv_wide = (staged(0, at + k * D, [C, P]) for k in (5, 6))

        S = bank("S", UNITS)
        O = bank("O", 2)
        PT = bank("PT", UNITS)
        PV = bank("PV", C)
        R1 = [bank(f"R1{n}", 4) for n in range(2)]
        R0 = bank("R0", 10)
        R2 = bank("R2", 12)

        weights_loaded = sem("weights_loaded")
        const_pool = sem("const_pool")
        const_dve = sem("const_dve")
        waits_taken = sem("waits_taken")
        const_pe = sem("const_pe")
        x0_loaded = [sem(f"x0_loaded{p}") for p in range(2)]
        stored = [sem(f"stored{p}") for p in range(2)]
        stats_done = [counter(f"stats_done{n}", GB) for n in range(4)]
        mv_done = [counter(f"mv_done{n}", GB) for n in range(4)]
        ln_small = [counter(f"ln_small{n}", 4 if n == 3 else 3) for n in range(4)]
        xhat0_ready = counter("xhat0_ready", GB)
        hT0_high = counter("hT0_high", C)
        hT0_low = counter("hT0_low", C)
        hT1_high = counter("hT1_high", C)
        hT2_high = counter("hT2_high", C)
        attT1_high = counter("attT1_high", C)
        xhat1_ready = counter("xhat1_ready", GB)
        xhat2_ready = counter("xhat2_ready", GB)
        h3_ready = counter("h3_ready", GB)
        relsq_ready = counter("relsq_ready", 1)
        rnorm_ready = counter("rnorm_ready", 1)
        x1_bias_ready = counter("x1_bias_ready", 1)
        k_wide_ready = counter("k_wide_ready", C)
        exps_ready = counter("exps_ready", UNITS)
        rsums_ready = counter("rsums_ready", UNITS)
        probs_ready = counter("probs_ready", UNITS)
        leaky_ready = counter("leaky_ready", 1)
        max2_ready = counter("max2_ready", 2)
        exp2_ready = counter("exp2_ready", 1)
        rsum2_ready = counter("rsum2_ready", 1)
        att2_ready = counter("att2_ready", 1)
        e_z_ready = counter("e_z_ready", 2)
        x3_ready = counter("x3_ready", 2)
        maxA_ready = counter("maxA_ready", 2)
        gain3_ready = counter("gain3_ready", 2)
        x4_ready = counter("x4_ready", GB)

        x_groups = x.rearrange("(g b) n d -> g n b d", b=GB)
        out_groups = out.rearrange("(g b) n d -> g n b d", b=GB)

        def rows(w):
            return w.rearrange("(c p) n -> p c n", p=P)

        def chunk_columns(tile, b):
            return [(tile[:, c:c + 1], b[c * P:(c + 1) * P].rearrange("(p o) -> p o", o=1)) for c in range(C)]

        def wide(b):
            return b.rearrange("(o n) -> o n", o=1).to_broadcast([P, b.shape[0]])

        WEIGHTS = [
            (adj_sb[:], adj), (w0q_in, rows(w0q)), (w0k_in, rows(w0k)), (w0v_in, rows(w0v)),
            (w1q_in, rows(w1q)), (w1k_in, rows(w1k)), (w1v_in, rows(w1v)), (w1o_in, rows(w1o)),
            *chunk_columns(bq_cols, b1q), *chunk_columns(bk_cols, b1k), *chunk_columns(bv_cols, b1v),
            (bo_rows, wide(b1o)), (w2_in[:, :, 0:D], rows(w2)),
            (a_rows, wide(a2.rearrange("f o -> (f o)"))), (beta_col[:], wide(beta2)),
            (b3_col[:], b3.rearrange("(p o) -> p o", o=1)),
        ]
        ALL_WEIGHTS = 16 * len(WEIGHTS)

        def apart(engine):
            engine.sem_inc(waits_taken, 1)

        def for_group(step):
            def run(g, n):
                if g.exists():
                    step(g, n)
            return run

        def iterations(engine, iteration):
            for i in range(STEADY.start):
                iteration(Group(0, i))
            assert STEADY.start % 2 == 0 and len(STEADY) % 2 == 0
            with engine.Fori(STEADY.start // 2, STEADY.stop // 2) as half:
                iteration(Group(half, 0))
                iteration(Group(half, 1))
            for i in range(STEADY.stop, ITERS):
                iteration(Group(0, i))

        block = ctx.enter_context(nc.Block())

        @block.sync
        def _(sp):
            for dst, src in WEIGHTS:
                sp.dma_start(dst, src).then_inc(weights_loaded, 16)

            def load(g):
                if counts(R0.drained.at(g.ahead(-2), 10)):
                    sp.wait_ge(R0.drained.sem, R0.drained.at(g.ahead(-2), 10))
                sp.dma_start(x0[g.parity][:], x_groups[g.index()]).then_inc(x0_loaded[g.parity], 16)

            def store(g):
                sp.wait_ge(x4_ready.sem, x4_ready.at(g, GB))
                sp.dma_start(out_groups[g.index()], x3[g.parity][:]).then_inc(stored[g.parity], 16)

            load(Group(0, 0))

            def iteration(i):
                g = i.ahead(1 - NORM0)
                if g.exists():
                    load(g)
                g = i.ahead(-LAYER3)
                if g.exists():
                    store(g)

            for i in range(STEADY.start):
                iteration(Group(0, i))
            with sp.Fori(STEADY.start // 2, STEADY.stop // 2 - 1) as half:
                iteration(Group(half, 0))
                iteration(Group(half, 1))
            for i in range(STEADY.stop - 2, ITERS):
                iteration(Group(0, i))
            for p in range(2):
                sp.wait_ge(stored[p], 16 * (NG // 2))

        @block.tensor
        def _(pe):
            mm, transpose = nc.tensor.matmul, nc.tensor.transpose

            pe.wait_ge(weights_loaded, ALL_WEIGHTS)
            pe.wait_ge(const_pool, 2)
            for c in range(C):
                for k in range(C):
                    last = mm(R0.tensor[:, c * D:(c + 1) * D], w0k_in[:, k, c * P:(c + 1) * P], w0q_in[:, k, :],
                              start=(k == 0), stop=(k == C - 1))
            last.then_inc(const_pe, 1)
            for c in range(C):
                for k in range(C):
                    last = transpose(R2.tensor[:, c * D + k * P:c * D + (k + 1) * P],
                                     w0v_in[:, k, c * P:(c + 1) * P], ident[:])
            last.then_inc(const_pe, 1)
            transpose(R1[0].tensor[:, 0:P], adj_sb[:], ident[:]).then_inc(const_pe, 1)
            pe.wait_ge(const_dve, CONST_BV)
            for c in range(C):
                last = mm(R1[1].tensor[:, 0:D], bv_wide[:, c, :], w1o_in[:, c, :], start=(c == 0), stop=(c == C - 1))
            last.then_inc(const_pe, 1)
            pe.wait_ge(const_dve, CONST_DVE)
            pe.wait_ge(const_pool, CONST_POOL)

            def fill(bank, g, k):
                if counts(bank.drained.at(g, k)):
                    pe.wait_ge(bank.drained.sem, bank.drained.at(g, k))

            def turn(bank, g, k, src, c):
                fill(bank, g, k)
                for b in range(GB):
                    last = transpose(bank.tensor[:, b * N:(b + 1) * N], src[:, b, c * P:(c + 1) * P], ident[:])
                last.then_inc(bank.filled.sem, 1)

            def product(dst, lhsT, rhs):
                steps = [(c, i, j) for c in range(C) for i, j in PASSES]
                for n, (c, i, j) in enumerate(steps):
                    last = mm(dst, lhsT(i, c), rhs(j, c), start=(n == 0), stop=(n == len(steps) - 1))
                return last

            def project_T(bank, g, k, w, hT, m):
                fill(bank, g, k)
                last = product(bank.tensor[:], lambda i, c: w[i][:, c, m * P:(m + 1) * P], lambda j, c: hT[j][:, c, :])
                last.then_inc(bank.filled.sem, 1)

            def project(bank, g, k, hT, w, half):
                fill(bank, g, k)
                for n, b in enumerate((2 * half, 2 * half + 1)):
                    last = product(bank.tensor[:, n * D:(n + 1) * D], lambda i, c: hT[i][:, c, b * N:(b + 1) * N],
                                   lambda j, c: w[j][:, c, :])
                last.then_inc(bank.filled.sem, 1)

            @for_group
            def layer0(g, step):
                if step < 2:
                    pe.wait_ge(xhat0_ready.sem, xhat0_ready.at(g, GB))
                    turn(R0, g, step, xhat0, step)
                elif step < 4:
                    pe.wait_ge(hT0_low.sem, hT0_low.at(g, C))
                    project_T(R0, g, step, A0, hT0_parts, step - 2)
                elif step == 4:
                    fill(R0, g, 4)
                    for b in range(GB):
                        s = slice(b * N, (b + 1) * N)
                        for c in range(C):
                            last = mm(R0.tensor[:, s], t0[:, c, s], hT0[:, c, s], start=(c == 0), stop=(c == C - 1))
                    last.then_inc(R0.filled.sem, 1)
                elif step < 7:
                    project(R0, g, step, hT0_parts, w0vT, step - 5)
                elif step == 7:
                    fill(R0, g, 7)
                    pe.wait_ge(relsq_ready.sem, relsq_ready.at(g, 1))
                    for b in range(GB):
                        s = slice(b * N, (b + 1) * N)
                        last = mm(R0.tensor[:, s], relsq[:, s], ones[:], start=True, stop=True)
                    last.then_inc(R0.filled.sem, 1)
                else:
                    fill(R0, g, step)
                    for n, b in enumerate((2 * (step - 8), 2 * (step - 8) + 1)):
                        last = mm(R0.tensor[:, n * D:(n + 1) * D], relT[:, b * N:(b + 1) * N], v0[:, b, :],
                                  start=True, stop=True)
                    last.then_inc(R0.filled.sem, 1)

            @for_group
            def turn1(g, c):
                pe.wait_ge(xhat1_ready.sem, xhat1_ready.at(g, GB))
                turn(R1[c], g, 0, xhat1, c)

            def both_hT1(g):
                for n in range(2):
                    pe.wait_ge(R1[n].drained.sem, R1[n].drained.at(g, 1))

            @for_group
            def keys(g, m):
                both_hT1(g)
                project_T(R1[m], g, 1, w1k_sb, hT1, m)

            @for_group
            def queries(g, m):
                project_T(R1[m], g, 2, w1q_sb, hT1, m)

            @for_group
            def values(g, half):
                project(R1[half], g, 3, hT1, w1v_sb, half)

            @for_group
            def scores(g, u):
                m, b = divmod(u, GB)
                fill(S, g, u)
                pe.wait_ge(k_wide_ready.sem, k_wide_ready.at(g, m + 1))
                pe.wait_ge(R1[m].drained.sem, R1[m].drained.at(g, 3))
                last = mm(S.tensor[:], qT[g.parity][:, m, b * N:(b + 1) * N],
                          k_wide[g.parity][:, m, b, :, :].rearrange("p h n -> p (h n)"), start=True, stop=True)
                last.then_inc(S.filled.sem, 1)

            @for_group
            def turn_probs(g, u):
                fill(PT, g, u)
                pe.wait_ge(probs_ready.sem, probs_ready.at(g, u + 1))
                for h in range(HQ):
                    last = transpose(PT.tensor[:, h * N:(h + 1) * N], probs[:, u % 4, h, :], ident[:])
                last.then_inc(PT.filled.sem, 1)

            @for_group
            def weigh_values(g, u):
                m, b = divmod(u, GB)
                if b == 0:
                    fill(PV, g, m)
                pe.wait_ge(PT.drained.sem, PT.drained.at(g, u + 1))
                if u == 0:
                    for n in range(2):
                        pe.wait_ge(R1[n].drained.sem, R1[n].drained.at(g, 4))
                for h in range(HQ):
                    last = mm(PV.tensor[h * HD:(h + 1) * HD, b * N:(b + 1) * N],
                              v1[g.parity][:, b, m * P + h * HD:m * P + (h + 1) * HD], probsT[:, u % 2, h, :],
                              start=True, stop=True, tile_position=(0, h * HD))
                if b == GB - 1:
                    last.then_inc(PV.filled.sem, 1)

            @for_group
            def project_out(g, half):
                pe.wait_ge(PV.drained.sem, PV.drained.at(g, C))
                project(O, g, half, attT1, w1o_sb, half)

            @for_group
            def layer2(g, step):
                if step < 2:
                    pe.wait_ge(xhat2_ready.sem, xhat2_ready.at(g, GB))
                    turn(R2, g, step, xhat2, step)
                elif step == 6:
                    fill(R2, g, 6)
                    last = product(R2.tensor[:], lambda i, c: wa2_wide[i][:, c, :], lambda j, c: hT2[j][:, c, :])
                    last.then_inc(R2.filled.sem, 1)
                elif step < 6:
                    b = step - 2
                    fill(R2, g, step)
                    last = product(R2.tensor[:, 0:D + 1], lambda i, c: hT2[i][:, c, b * N:(b + 1) * N],
                                   lambda j, c: w2_aug[j][:, c, :])
                    last.then_inc(R2.filled.sem, 1)
                elif step == 7:
                    fill(R2, g, 7)
                    pe.wait_ge(att2_ready.sem, att2_ready.at(g, 1))
                    for b in range(GB):
                        last = transpose(R2.tensor[:, b * N:(b + 1) * N], att2b[:, b, :], ident[:])
                    last.then_inc(R2.filled.sem, 1)
                else:
                    fill(R2, g, step)
                    for n, b in enumerate((2 * (step - 8), 2 * (step - 8) + 1)):
                        last = mm(R2.tensor[:, n * D:(n + 1) * D], att2T[:, b, :], hp[:, b, 0:D], start=True, stop=True)
                    last.then_inc(R2.filled.sem, 1)

            @for_group
            def layer3(g, half):
                pe.wait_ge(h3_ready.sem, h3_ready.at(g, 2 * half + 2))
                fill(R2, g, 10 + half)
                last = mm(R2.tensor[:], adj_T[:],
                          h3[:, 2 * half:2 * half + 2, :].rearrange("p b d -> p (b d)"), start=True, stop=True)
                last.then_inc(R2.filled.sem, 1)

            def iteration(i):
                n0, g0, gp, g1, g2, g3 = (i.ahead(-s) for s in (NORM0, LAYER0, PROJ1, ATTN1, LAYER2, LAYER3))
                project_out(g2, 1)
                turn_probs(g1, 1)
                queries(gp, 1)

                scores(g1, 5)
                weigh_values(g1, 0)
                layer0(g0, 5)
                turn_probs(g1, 2)
                layer3(g3, 0)
                layer0(g0, 6)
                weigh_values(g1, 1)
                layer3(g3, 1)
                layer0(g0, 7)
                layer2(g2, 0)
                turn_probs(g1, 3)

                scores(g1, 6)
                values(gp, 0)
                layer2(g2, 1)

                scores(g1, 7)
                layer0(g0, 8)
                layer2(g2, 2)
                weigh_values(g1, 2)
                turn_probs(g1, 4)
                layer2(g2, 3)
                layer0(g0, 9)

                scores(gp, 0)
                layer2(g2, 4)
                weigh_values(g1, 3)
                layer0(n0, 0)
                layer2(g2, 5)
                values(gp, 1)
                layer2(g2, 6)
                turn_probs(g1, 5)
                weigh_values(g1, 4)
                layer0(n0, 1)
                turn_probs(g1, 6)
                weigh_values(g1, 5)
                turn1(g0, 0)
                turn1(g0, 1)
                turn_probs(g1, 7)

                scores(gp, 1)
                weigh_values(g1, 6)
                keys(g0, 0)
                keys(g0, 1)
                layer2(g2, 7)

                scores(gp, 2)
                layer2(g2, 8)
                weigh_values(g1, 7)

                scores(gp, 3)
                layer0(n0, 2)
                turn_probs(gp, 0)
                layer2(g2, 9)
                layer0(n0, 3)
                project_out(g1, 0)
                layer0(n0, 4)

                scores(gp, 4)
                queries(g0, 0)

            iterations(pe, iteration)

        @block.scalar
        def _(act):
            activation = nc.scalar.activation

            def copy_out(bank, g, k, dst, src=None, func=ACT.Copy, **kw):
                act.wait_ge(bank.filled.sem, bank.filled.at(g, k + 1))
                activation(dst, bank.tensor[:] if src is None else src, func, **kw)\
                    .then_inc(bank.drained.sem, 1)

            def high_out(bank, g, k, dst, ready, func):
                act.wait_ge(bank.filled.sem, bank.filled.at(g, k + 1))
                activation(dst, bank.tensor[:], func).then_inc(ready.sem, 1)

            @for_group
            def norm3(g, _):
                act.wait_ge(ln_small[3].sem, ln_small[3].at(g, 4))
                if counts(R2.filled.at(g, 0)):
                    act.wait_ge(R2.filled.sem, R2.filled.at(g, 0))
                for b in range(GB):
                    activation(h3[:, b, :], x3[g.parity][:, b, :], ACT.Relu, bias=shift[3][:, b:b + 1],
                               scale=rstd[3][:, b:b + 1]).then_inc(h3_ready.sem, 1)

            @for_group
            def layer0(g, k):
                if k < 2:
                    copy_out(R0, g, k, hT0[:, k, :], func=ACT.Relu)
                elif k < 4:
                    copy_out(R0, g, k, t0[:, k - 2, :])
                else:
                    half = k - 5
                    copy_out(R0, g, k, v0[:, 2 * half:2 * half + 2, :].rearrange("p b d -> p (b d)"))

            @for_group
            def relu_hT1(g, c):
                high_out(R1[c], g, 0, hT1[0][:, c, :], hT1_high, ACT.Relu)

            @for_group
            def queries(g, m):
                copy_out(R1[m], g, 2, qT[g.parity][:, m, :], func=ACT.Identity, bias=bq_scaled[:, m:m + 1], scale=HD ** -0.5)

            @for_group
            def values(g, half):
                copy_out(R1[half], g, 3, v1[g.parity][:, 2 * half:2 * half + 2, :].rearrange("p b d -> p (b d)"))

            @for_group
            def exps(g, u):
                act.wait_ge(S.drained.sem, S.drained.at(g, u + 1))
                for h in range(HQ):
                    last = activation(probs[:, u % 4, h, :], scores1[:, u % 2, h, :], ACT.Exp, scale=-1.0,
                                      bias=negmax[:, u, h:h + 1], accum_out=sums[:, u, h:h + 1])
                last.then_inc(exps_ready.sem, 1)

            @for_group
            def probs_out(g, u):
                copy_out(PT, g, u, probsT[:, u % 2, :, :].rearrange("p h n -> p (h n)"))

            @for_group
            def attention_out(g, m):
                high_out(PV, g, m, attT1[0][:, m, :], attT1_high, ACT.Copy)

            @for_group
            def layer2(g, k):
                if k < 2:
                    high_out(R2, g, k, hT2[0][:, k, :], hT2_high, ACT.Relu)
                elif k < 6:
                    copy_out(R2, g, k, hp[:, k - 2, :], src=R2.tensor[:, 0:D + 1])
                elif k == 6:
                    act.wait_ge(R2.filled.sem, R2.filled.at(g, 7))
                    act.wait_ge(R2.drained.sem, R2.drained.at(g, 6))
                    for b in range(GB):
                        last = activation(e_sum[:, b, :], R2.tensor[:, b * N:(b + 1) * N], ACT.Identity,
                                          bias=hp[:, b, D:D + 1])
                    last.then_inc(R2.drained.sem, 1)
                elif k == 7:
                    copy_out(R2, g, 7, att2T[:].rearrange("p b n -> p (b n)"))
                else:
                    half = k - 8
                    act.wait_ge(R2.filled.sem, R2.filled.at(g, k + 1))
                    activation(e_z[:, 2 * half:2 * half + 2, :].rearrange("p b d -> p (b d)"), R2.tensor[:], ACT.Exp)\
                        .then_inc(e_z_ready.sem, 1)

            @for_group
            def softmax2(g, _):
                act.wait_ge(max2_ready.sem, max2_ready.at(g, 2))
                for b in range(GB):
                    last = activation(att2[:, b, :], e_masked[:, b, :], ACT.Exp, bias=negmax2[:, b:b + 1],
                                      accum_out=sum2[:, b:b + 1])
                last.then_inc(exp2_ready.sem, 1)

            act.wait_ge(const_dve, CONST_DVE)

            def iteration(i):
                n0, g0, gp, g1, g2, g3 = (i.ahead(-s) for s in (NORM0, LAYER0, PROJ1, ATTN1, LAYER2, LAYER3))

                exps(g1, 3)

                exps(g1, 4)
                norm3(g3, 0)
                layer0(g0, 5)
                layer0(g0, 6)
                probs_out(g1, 2)

                exps(g1, 5)
                queries(gp, 0)
                layer2(g2, 0)
                layer2(g2, 1)

                exps(g1, 6)
                layer2(g2, 2)
                probs_out(g1, 4)
                queries(gp, 1)
                layer2(g2, 3)
                layer2(g2, 4)
                values(gp, 0)
                layer2(g2, 5)
                attention_out(g1, 0)
                layer0(n0, 0)

                exps(g1, 7)
                layer2(g2, 6)
                layer0(n0, 1)
                probs_out(g1, 6)
                relu_hT1(g0, 0)
                relu_hT1(g0, 1)
                softmax2(g2, 0)

                exps(gp, 0)
                layer2(g2, 7)

                exps(gp, 1)
                layer2(g2, 8)

                exps(gp, 2)
                attention_out(g1, 1)
                layer0(n0, 2)
                layer2(g2, 9)
                probs_out(gp, 0)
                layer0(n0, 3)

            iterations(act, iteration)

        @block.vector
        def _(dve):
            v = nc.vector
            built = [0]

            def constant(instruction):
                instruction.then_inc(const_dve, 1)
                built[0] += 1
                dve.wait_ge(const_dve, built[0])

            def split(parts, value):
                constant(v.tensor_copy(parts[0][:], value))
                constant(v.tensor_tensor(parts[1][:], value, parts[0][:], ALU.subtract))

            dve.wait_ge(weights_loaded, ALL_WEIGHTS)
            dve.wait_ge(const_pool, 3)
            for c in range(C):
                constant(v.tensor_scalar(bv_wide[:, c, :], ones[:], bv_cols[:, c:c + 1], None, ALU.mult))
            assert built[0] == CONST_BV
            constant(v.tensor_scalar(one_minus_adj[:, 0:P], adj_sb[:], -1.0, 1.0, ALU.mult, ALU.add))
            constant(v.tensor_scalar(mask1[:], one_minus_adj[:, 0:P], -1e9, None, ALU.mult))
            constant(v.tensor_scalar(bq_scaled[:], bq_cols[:], HD ** -0.5, None, ALU.mult))
            for c in range(C):
                for half, col in enumerate((w2_in[:, c, D:D + 1], wa2[:, c:c + 1])):
                    constant(v.tensor_tensor_reduce(wa_junk, w2_in[:, c, 0:D], a_rows[:, half * D:(half + 1) * D],
                                                    1.0, 0.0, ALU.mult, ALU.add, col))
                constant(v.tensor_scalar(wa2_in[:, c, :], ones[:], wa2[:, c:c + 1], None, ALU.mult))
            constant(v.tensor_scalar(beta_eye[:], ident[:], beta_col[:, 0:1], None, ALU.mult))
            for parts, value in ((w1q_sb, w1q_in), (w1k_sb, w1k_in), (w1v_sb, w1v_in), (w1o_sb, w1o_in),
                                 (w2_aug, w2_in), (wa2_wide, wa2_in)):
                split(parts, value)
            dve.wait_ge(const_pe, 1)
            split(A0, R0.tensor[:].rearrange("p (c d) -> p c d", c=C))
            dve.wait_ge(const_pe, 2)
            split(w0vT, R2.tensor[:].rearrange("p (c d) -> p c d", c=C))
            dve.wait_ge(const_pe, 3)
            constant(v.tensor_copy(adj_T[:], R1[0].tensor[:, 0:P]))
            dve.wait_ge(const_pe, 4)
            constant(v.tensor_tensor(bias1[:], R1[1].tensor[:, 0:D], bo_rows, ALU.add))
            assert built[0] == CONST_DVE

            def copy_out(bank, g, k, dst):
                dve.wait_ge(bank.filled.sem, bank.filled.at(g, k + 1))
                v.tensor_copy(dst, bank.tensor[:]).then_inc(bank.drained.sem, 1)

            def low_out(bank, g, k, parts, c, ready):
                dve.wait_ge(ready.sem, ready.at(g, c + 1))
                v.scalar_tensor_tensor(parts[1][:, c, :], bank.tensor[:], 0.0, parts[0][:, c, :],
                                       ALU.max, ALU.subtract).then_inc(bank.drained.sem, 1)

            def statistics(n, g, src, batches, last):
                for b in batches:
                    v.bn_stats(stats[n][:, b, :], src[:, b, :]).then_inc(stats_done[n].sem, 1)
                if last:
                    if counts(ln_small[n].at(g, 0)):
                        dve.wait_ge(ln_small[n].sem, ln_small[n].at(g, 0))
                    for b in range(GB):
                        dve.wait_ge(stats_done[n].sem, stats_done[n].at(g, b + 1))
                        apart(dve)
                        v.bn_aggr(mv[n][:, b, :], stats[n][:, b, :]).then_inc(mv_done[n].sem, 1)

            @for_group
            def norm0(g, _):
                dve.wait_ge(x0_loaded[g.parity], g.pair_times(16, 16))
                statistics(0, g, x0[g.parity], range(GB), True)

            @for_group
            def layer0(g, k):
                if k < 2:
                    dve.wait_ge(R0.drained.sem, R0.drained.at(g, k + 1))
                    v.tensor_copy(hT0_parts[0][:, k, :], hT0[:, k, :]).then_inc(hT0_high.sem, 1)
                elif k == 4:
                    dve.wait_ge(R0.filled.sem, R0.filled.at(g, 5))
                    v.tensor_tensor(relT[:].rearrange("p (b n) -> p b n", b=GB),
                                    R0.tensor[:].rearrange("p (b n) -> p b n", b=GB),
                                    adj_sb[:].unsqueeze(1).to_broadcast([P, GB, N]), ALU.mult)\
                        .then_inc(R0.drained.sem, 1)
                elif k == 7:
                    dve.wait_ge(R0.filled.sem, R0.filled.at(g, 8))
                    if counts(rnorm_ready.at(g, 0)):
                        dve.wait_ge(rnorm_ready.sem, rnorm_ready.at(g, 0))
                    v.tensor_copy(normsq[:], R0.tensor[:, 0:COLS:N]).then_inc(R0.drained.sem, 1)
                else:
                    half = k - 8
                    dve.wait_ge(R0.filled.sem, R0.filled.at(g, k + 1))
                    if half == 0:
                        dve.wait_ge(rnorm_ready.sem, rnorm_ready.at(g, 1))
                        if counts(xhat1_ready.at(g, 0)):
                            dve.wait_ge(xhat1_ready.sem, xhat1_ready.at(g, 0))
                        if counts(x1_bias_ready.at(g.ahead(-1), 0)):
                            dve.wait_ge(x1_bias_ready.sem, x1_bias_ready.at(g.ahead(-1), 0))
                    for n, b in enumerate((2 * half, 2 * half + 1)):
                        last = v.scalar_tensor_tensor(x1[g.parity][:, b, :], R0.tensor[:, n * D:(n + 1) * D],
                                                      rnorm[:, b:b + 1], x0[g.parity][:, b, :], ALU.mult, ALU.add)
                    last.then_inc(R0.drained.sem, 1)

            @for_group
            def norm1(g, _):
                dve.wait_ge(R0.drained.sem, R0.drained.at(g, 10))
                statistics(1, g, x1[g.parity], range(GB), True)

            @for_group
            def relu_hT1(g, c):
                low_out(R1[c], g, 0, hT1, c, hT1_high)

            @for_group
            def keys(g, m):
                dve.wait_ge(R1[m].filled.sem, R1[m].filled.at(g, 2))
                if counts(k_wide_ready.at(g, 0)):
                    dve.wait_ge(k_wide_ready.sem, k_wide_ready.at(g, 0))
                v.tensor_scalar(kT[:, m, :], R1[m].tensor[:], bk_cols[:, m:m + 1], None, ALU.add)\
                    .then_inc(R1[m].drained.sem, 1)

            @for_group
            def values(g, half):
                copy_out(R1[half], g, 3, v1[g.parity][:, 2 * half:2 * half + 2, :].rearrange("p b d -> p (b d)"))

            @for_group
            def maxima(g, u):
                dve.wait_ge(S.filled.sem, S.filled.at(g, u + 1))
                if counts(exps_ready.at(g.ahead(-1), UNITS + u - 1)):
                    dve.wait_ge(exps_ready.sem, exps_ready.at(g.ahead(-1), UNITS + u - 1))
                apart(dve)
                for h in range(HQ):
                    last = v.tensor_tensor_reduce(scores1[:, u % 2, h, :], S.tensor[:, h * N:(h + 1) * N], mask1[:],
                                                  -1.0, BIG, ALU.add, ALU.min, negmax[:, u, h:h + 1])
                last.then_inc(S.drained.sem, 1)

            @for_group
            def invert_sums(g, u):
                dve.wait_ge(exps_ready.sem, exps_ready.at(g, u + 1))
                if counts(probs_ready.at(g.ahead(-1), u + 1)):
                    dve.wait_ge(probs_ready.sem, probs_ready.at(g.ahead(-1), u + 1))
                v.reciprocal(rsums[:, u, :], sums[:, u, :]).then_inc(rsums_ready.sem, 1)

            @for_group
            def probs_out(g, u):
                copy_out(PT, g, u, probsT[:, u % 2, :, :].rearrange("p h n -> p (h n)"))

            @for_group
            def attention_out(g, m):
                dve.wait_ge(attT1_high.sem, attT1_high.at(g, m + 1))
                v.tensor_tensor(attT1[1][:, m, :], PV.tensor[:], attT1[0][:, m, :], ALU.subtract)\
                    .then_inc(PV.drained.sem, 1)

            @for_group
            def residual1(g, half):
                dve.wait_ge(O.filled.sem, O.filled.at(g, half + 1))
                dve.wait_ge(x1_bias_ready.sem, x1_bias_ready.at(g, 1))
                if half == 0:
                    if counts(xhat2_ready.at(g, 0)):
                        dve.wait_ge(xhat2_ready.sem, xhat2_ready.at(g, 0))
                rows_ = slice(2 * half, 2 * half + 2)
                v.tensor_tensor(x2[g.parity][:, rows_, :].rearrange("p b d -> p (b d)"), O.tensor[:],
                                x1_bias[g.parity][:, rows_, :].rearrange("p b d -> p (b d)"), ALU.add)\
                    .then_inc(O.drained.sem, 1)
                dve.wait_ge(O.drained.sem, O.drained.at(g, half + 1))
                statistics(2, g, x2[g.parity], (2 * half, 2 * half + 1), half == 1)

            @for_group
            def layer2(g, k):
                if k < 2:
                    low_out(R2, g, k, hT2, k, hT2_high)
                else:
                    dve.wait_ge(R2.drained.sem, R2.drained.at(g, 7))
                    v.scalar_tensor_tensor(e_leaky[:], e_sum[:], ALPHA, e_sum[:], ALU.mult, ALU.max)\
                        .then_inc(leaky_ready.sem, 1)
                    dve.wait_ge(leaky_ready.sem, leaky_ready.at(g, 1))
                    if counts(exp2_ready.at(g, 0)):
                        dve.wait_ge(exp2_ready.sem, exp2_ready.at(g, 0))
                    apart(dve)
                    for b in range(GB):
                        last = v.tensor_tensor_reduce(e_masked[:, b, :], e_leaky[:, b, :], adj_sb[:], 1.0, -3.4e38,
                                                      ALU.mult, ALU.max, max2[:, b:b + 1])
                    last.then_inc(max2_ready.sem, 1)
                    dve.wait_ge(max2_ready.sem, max2_ready.at(g, 1))
                    v.tensor_scalar(negmax2[:], max2[:], -1.0, None, ALU.mult).then_inc(max2_ready.sem, 1)

            @for_group
            def weights2(g, _):
                dve.wait_ge(exp2_ready.sem, exp2_ready.at(g, 1))
                v.reciprocal(rsum2[:], sum2[:]).then_inc(rsum2_ready.sem, 1)
                dve.wait_ge(rsum2_ready.sem, rsum2_ready.at(g, 1))
                for b in range(GB):
                    last = v.scalar_tensor_tensor(att2b[:, b, :], att2[:, b, :], rsum2[:, b:b + 1], beta_eye[:],
                                                  ALU.mult, ALU.add)
                last.then_inc(att2_ready.sem, 1)

            @for_group
            def elu(g, half):
                rows_ = slice(2 * half, 2 * half + 2)
                flat = lambda t: t[:, rows_, :].rearrange("p b d -> p (b d)")
                dve.wait_ge(e_z_ready.sem, e_z_ready.at(g, half + 1))
                last = v.scalar_tensor_tensor(flat(x2[g.parity]), R2.tensor[:], 0.0, flat(x2[g.parity]),
                                              ALU.max, ALU.add)
                last.then_inc(R2.drained.sem, 1)
                if counts(R2.drained.at(g, 9 + half)):
                    dve.wait_ge(R2.drained.sem, R2.drained.at(g, 9 + half))
                if half == 0:
                    if counts(g.pair_times(16)):
                        dve.wait_ge(stored[g.parity], g.pair_times(16))
                v.scalar_tensor_tensor(flat(x3[g.parity]), flat(e_z), 1.0, flat(x2[g.parity]), ALU.min, ALU.add)\
                    .then_inc(x3_ready.sem, 1)
                dve.wait_ge(x3_ready.sem, x3_ready.at(g, half + 1))
                statistics(3, g, x3[g.parity], (2 * half, 2 * half + 1), half == 1)

            @for_group
            def layer3(g, half):
                if counts(R2.filled.at(g, 11 + half)):
                    dve.wait_ge(R2.filled.sem, R2.filled.at(g, 11 + half))
                v.tensor_reduce(maxA[:, 2 * half:2 * half + 2], R2.tensor[:].rearrange("p (b n) -> p b n", b=2),
                                AX.X, ALU.max).then_inc(R2.drained.sem, 1)
                if half == 1:
                    dve.wait_ge(R2.drained.sem, R2.drained.at(g, 12))
                    v.tensor_scalar(gain3[:], maxA[:], b3_col[:, 0:1], 0.0, ALU.add, ALU.max)\
                        .then_inc(gain3_ready.sem, 1)
                    dve.wait_ge(gain3_ready.sem, gain3_ready.at(g, 1))
                    if counts(x4_ready.at(g, 0)):
                        dve.wait_ge(x4_ready.sem, x4_ready.at(g, 0))
                    v.tensor_scalar(gain3m[:], gain3[:], -1.0, None, ALU.add).then_inc(gain3_ready.sem, 1)

            def iteration(i):
                n0, g0, gp, g1, g2, g3 = (i.ahead(-s) for s in (NORM0, LAYER0, PROJ1, ATTN1, LAYER2, LAYER3))

                maxima(g1, 4)
                layer0(g0, 4)
                residual1(g2, 1)
                invert_sums(g1, 3)
                probs_out(g1, 1)

                maxima(g1, 5)
                layer3(g3, 0)
                norm0(n0, 0)
                layer3(g3, 1)
                layer0(g0, 7)
                layer2(g2, 0)
                invert_sums(g1, 4)

                maxima(g1, 6)
                probs_out(g1, 3)
                layer2(g2, 1)

                maxima(g1, 7)
                layer0(g0, 8)
                invert_sums(g1, 5)
                layer0(g0, 9)
                invert_sums(g1, 6)
                norm1(g0, 0)

                maxima(gp, 0)
                attention_out(g1, 0)
                layer0(n0, 0)
                values(gp, 1)
                invert_sums(g1, 7)
                probs_out(g1, 5)
                layer2(g2, 7)
                relu_hT1(g0, 0)
                relu_hT1(g0, 1)

                maxima(gp, 1)
                weights2(g2, 0)
                layer0(n0, 1)
                probs_out(g1, 7)
                invert_sums(gp, 0)
                keys(g0, 0)

                maxima(gp, 2)
                keys(g0, 1)
                elu(g2, 0)

                maxima(gp, 3)
                attention_out(g1, 1)
                invert_sums(gp, 1)
                elu(g2, 1)
                residual1(g1, 0)
                invert_sums(gp, 2)

            iterations(dve, iteration)

        @block.gpsimd
        def _(pool):
            p = nc.gpsimd
            p.memset(ident[:], 0.0).then_inc(const_pool, 1)
            pool.wait_ge(const_pool, 1)
            p.affine_select(out=ident[:], in_=ident[:], compare_op=ALU.not_equal, fill=1.0, base=0,
                            pattern=[[-1, P]], channel_multiplier=1).then_inc(const_pool, 1)
            p.memset(ones[:], 1.0).then_inc(const_pool, 1)
            p.memset(minus_half[:], -0.5).then_inc(const_pool, 1)
            p.memset(head_rows[:], 1.0).then_inc(const_pool, 1)
            for base, sign in ((0, 1), (HD - 1, -1)):
                pool.wait_ge(const_pool, 5 if sign > 0 else 6)
                p.affine_select(out=head_rows[:], in_=head_rows[:], compare_op=ALU.is_ge, fill=0.0, base=base,
                                pattern=[[-sign * HD, HQ]], channel_multiplier=sign).then_inc(const_pool, 1)
            pool.wait_ge(const_pool, CONST_POOL)
            pool.wait_ge(const_dve, CONST_DVE)

            def small(n, g):
                pool.wait_ge(mv_done[n].sem, mv_done[n].at(g, GB))
                apart(pool)
                p.tensor_scalar(veps[n][:], mv[n][:, :, 1], EPS, 1.0, ALU.add, ALU.mult)\
                    .then_inc(ln_small[n].sem, 1)
                p.tensor_scalar(negmean[n][:], mv[n][:, :, 0], -1.0, 0.0, ALU.mult, ALU.add)\
                    .then_inc(ln_small[n].sem, 1)
                pool.wait_ge(ln_small[n].sem, ln_small[n].at(g, 1))
                if n == 3:
                    if counts(h3_ready.at(g, 0)):
                        pool.wait_ge(h3_ready.sem, h3_ready.at(g, 0))
                p.tensor_tensor(rstd[n][:], veps[n][:], minus_half[:], ALU.pow).then_inc(ln_small[n].sem, 1)
                pool.wait_ge(ln_small[n].sem, ln_small[n].at(g, 3))
                if n == 3:
                    p.tensor_tensor(shift[n][:], negmean[n][:], rstd[n][:], ALU.mult).then_inc(ln_small[n].sem, 1)

            def normalise(n, g, dst, src, ready):
                small(n, g)
                apart(pool)
                for b in range(GB):
                    p.tensor_scalar(dst[:, b, :], src[:, b, :], negmean[n][:, b:b + 1], rstd[n][:, b:b + 1],
                                    ALU.add, ALU.mult).then_inc(ready.sem, 1)

            @for_group
            def norm0(g, _):
                if counts(R0.filled.at(g.ahead(-1), 2)):
                    pool.wait_ge(R0.filled.sem, R0.filled.at(g.ahead(-1), 2))
                normalise(0, g, xhat0, x0[g.parity], xhat0_ready)

            @for_group
            def norm1(g, _):
                if counts(R1[1].filled.at(g.ahead(-1), 1)):
                    pool.wait_ge(R1[1].filled.sem, R1[1].filled.at(g.ahead(-1), 1))
                normalise(1, g, xhat1, x1[g.parity], xhat1_ready)

            @for_group
            def norm2(g, _):
                if counts(R2.filled.at(g.ahead(-1), 2)):
                    pool.wait_ge(R2.filled.sem, R2.filled.at(g.ahead(-1), 2))
                normalise(2, g, xhat2, x2[g.parity], xhat2_ready)

            @for_group
            def norm3(g, _):
                small(3, g)

            @for_group
            def bias(g, _):
                if counts(O.drained.at(g.ahead(-1), 0)):
                    pool.wait_ge(O.drained.sem, O.drained.at(g.ahead(-1), 0))
                pool.wait_ge(R0.drained.sem, R0.drained.at(g, 10))
                p.tensor_tensor(x1_bias[g.parity][:], x1[g.parity][:],
                                bias1[:].unsqueeze(1).to_broadcast([P, GB, D]), ALU.add)\
                    .then_inc(x1_bias_ready.sem, 1)

            @for_group
            def low_hT0(g, c):
                pool.wait_ge(hT0_high.sem, hT0_high.at(g, c + 1))
                p.tensor_tensor(hT0_parts[1][:, c, :], hT0[:, c, :], hT0_parts[0][:, c, :], ALU.subtract)\
                    .then_inc(hT0_low.sem, 1)

            @for_group
            def squares(g, _):
                pool.wait_ge(R0.drained.sem, R0.drained.at(g, 5))
                p.tensor_tensor(relsq[:], relT[:], relT[:], ALU.mult).then_inc(relsq_ready.sem, 1)

            @for_group
            def invert_norm(g, _):
                pool.wait_ge(R0.drained.sem, R0.drained.at(g, 8))
                p.tensor_tensor(rnorm[:], normsq[:], minus_half[:], ALU.pow).then_inc(rnorm_ready.sem, 1)

            @for_group
            def widen_keys(g, m):
                pool.wait_ge(R1[m].drained.sem, R1[m].drained.at(g, 2))
                if counts(S.filled.at(g.ahead(-1), 0)):
                    pool.wait_ge(S.filled.sem, S.filled.at(g.ahead(-1), 0))
                apart(pool)
                for h in range(HQ):
                    last = p.tensor_scalar(k_wide[g.parity][:, m, :, h, :], kT[:, m, :].rearrange("p (b n) -> p b n", b=GB),
                                           head_rows[:, h:h + 1], 0.0, ALU.mult, ALU.add)
                last.then_inc(k_wide_ready.sem, 1)

            @for_group
            def normalise_probs(g, u):
                pool.wait_ge(rsums_ready.sem, rsums_ready.at(g, u + 1))
                p.tensor_tensor(probs[:, u % 4, :, :], probs[:, u % 4, :, :],
                                rsums[:, u, :].unsqueeze(2).to_broadcast([P, HQ, N]), ALU.mult)\
                    .then_inc(probs_ready.sem, 1)

            @for_group
            def residual3(g, _):
                pool.wait_ge(gain3_ready.sem, gain3_ready.at(g, 2))
                apart(pool)
                for b in range(GB):
                    p.tensor_scalar(x3[g.parity][:, b, :], x3[g.parity][:, b, :], 1.0, gain3m[:, b:b + 1],
                                    ALU.mult, ALU.add).then_inc(x4_ready.sem, 1)

            def iteration(i):
                n0, g0, gp, g1, g2, g3 = (i.ahead(-s) for s in (NORM0, LAYER0, PROJ1, ATTN1, LAYER2, LAYER3))

                normalise_probs(g1, 1)

                normalise_probs(g1, 2)
                norm3(g3, 0)
                squares(g0, 0)

                normalise_probs(g1, 3)
                norm2(g2, 0)
                bias(g1, 0)
                widen_keys(gp, 0)
                invert_norm(g0, 0)

                normalise_probs(g1, 4)
                norm0(n0, 0)

                normalise_probs(g1, 5)

                normalise_probs(g1, 6)
                norm1(g0, 0)

                normalise_probs(g1, 7)
                widen_keys(gp, 1)
                low_hT0(n0, 0)
                residual3(g3, 0)
                low_hT0(n0, 1)

                normalise_probs(gp, 0)

            iterations(pool, iteration)


CONST_BV, CONST_DVE, CONST_POOL = C, 30, 7

_INS = ["x", "adj", "L0_gnn_Wq", "L0_gnn_Wk", "L0_gnn_Wv", "L1_gnn_Wq", "L1_gnn_bq", "L1_gnn_Wk", "L1_gnn_bk",
        "L1_gnn_Wv", "L1_gnn_bv", "L1_gnn_Wo", "L1_gnn_bo", "L2_gnn_W", "L2_gnn_a", "L2_gnn_beta", "L3_gnn_b"]


def kernel(**inputs):
    import concourse.bacc as bacc
    from concourse.bass_utils import run_bass_kernel_spmd

    nc = bacc.Bacc("TRN2", target_bir_lowering=False, num_devices=1)
    arrays, args = {}, []
    for name in _INS:
        a = np.ascontiguousarray(inputs[name])
        arrays[f"in_{name}"] = a
        args.append(nc.dram_tensor(f"in_{name}", a.shape, mybir.dt.from_np(a.dtype), kind="ExternalInput").ap())
    args.append(nc.dram_tensor("out", (B, N, D), F32, kind="ExternalOutput").ap())
    build(nc, *args)
    r = run_bass_kernel_spmd(nc, [arrays], core_ids=[0])
    return r.results[0]["out"]
```

```python
from contextlib import ExitStack

import numpy as np

import concourse.bass as bass
from concourse import mybir
from concourse.alu_op_type import AluOpType as ALU

F32, F16 = mybir.dt.float32, mybir.dt.float16
ACT = mybir.ActivationFunctionType
AX = mybir.AxisListType

B, N, D = 128, 128, 256
P = 128
GB = 4
NG = B // GB
C = D // P
COLS = GB * N
H, HD = 8, 32
HQ = P // HD
UNITS = C * GB
EPS = 1e-5
ALPHA = 0.2
BIG = 3.4e38
H_SCALE, W_NORM = 64.0, 2048.0
T_SCALE = V_SCALE = H_SCALE
S2_SCALE = 16.0
SCALED = ("A0", "w0v", "w1q", "w1k", "w1v", "w1o", "w2", "wa")
SQUARES_MIN, SQUARES_MAX = 1e-36, 1e36
PASSES = ((0, 0), (0, 1), (1, 0))

LAST = 5
STEADY = range(LAST + 1, NG)
ITERS = NG + LAST


class Group:

    def __init__(self, half, odd):
        self.half, self.odd = half, odd

    def ahead(self, n):
        return Group(self.half, self.odd + n)

    @property
    def parity(self):
        return self.odd % 2

    def times(self, k, plus=0):
        return self.half * (2 * k) + (self.odd * k + plus)

    def pair_times(self, k, plus=0):
        return self.half * k + ((self.odd // 2) * k + plus)

    def index(self):
        return self.half * 2 + self.odd

    def first(self):
        return isinstance(self.half, int) and self.index() == 0

    def exists(self):
        return not isinstance(self.half, int) or 0 <= 2 * self.half + self.odd < NG


def counts(value):
    return not isinstance(value, int) or value > 0


class Counter:

    def __init__(self, semaphore, per_group):
        self.sem, self.per_group = semaphore, per_group

    def at(self, g, k):
        return g.times(self.per_group, k)


class Bank:

    def __init__(self, tensor, filled, drained, per_group):
        self.tensor = tensor
        self.filled, self.drained = Counter(filled, per_group), Counter(drained, per_group)


def build(nc, x, adj, w0q, w0k, w0v, w1q, b1q, w1k, b1k, w1v, b1v, w1o, b1o, w2, a2, beta2, b3, out):
    ctx = ExitStack()
    with ctx:
        def sb(name, shape, dt=F32):
            return ctx.enter_context(nc.sbuf_tensor(name, shape, dt))

        def pair(name, shape):
            return [sb(f"{name}_{part}", shape, F16) for part in ("high", "low")]

        def sem(name):
            return ctx.enter_context(nc.semaphore(name))

        def counter(name, per_group):
            return Counter(sem(name), per_group)

        def bank(name, per_group):
            t = ctx.enter_context(nc.psum_tensor(name, [P, COLS], F32))
            return Bank(t, sem(name + "_filled"), sem(name + "_drained"), per_group)

        ident = sb("ident", [P, P])
        mask1 = sb("mask1", [P, P])
        adj_sb = sb("adj_sb", [P, P])
        adj_T = sb("adj_T", [P, P])
        ones = sb("ones", [P, P])
        minus_half = sb("minus_half", [P, GB])
        head_rows = sb("head_rows", [P, HQ])
        A0 = pair("A0", [P, C, D])
        w0vT = pair("w0vT", [P, C, D])
        w1q_sb, w1k_sb, w1v_sb, w1o_sb = (pair(n, [P, C, D]) for n in ("w1q", "w1k", "w1v", "w1o"))
        bq_cols, bk_cols, bv_cols = (sb(n, [P, C]) for n in ("bq_cols", "bk_cols", "bv_cols"))
        bq_scaled = sb("bq_scaled", [P, C])
        bias1 = sb("bias1", [P, D])
        w2_aug = pair("w2_aug", [P, C, D + 2])
        ident_half = sb("ident_half", [P, P], F16)
        ones_half = sb("ones_half", [P, P], F16)
        w_squares, w_total, w_rnorm, w_power, w_scale, w_unscale, w_span, w_part = (
            sb(n, [P, len(SCALED)]) for n in ("w_squares", "w_total", "w_rnorm", "w_power", "w_scale", "w_unscale",
                                              "w_span", "w_part"))
        q_unscale, v0_unscale, k_unscale, out_unscale, hp_unscale, e_scale, minus_e_scale, s2_scale, s2_unscale = (
            sb(n, [P, 1]) for n in ("q_unscale", "v0_unscale", "k_unscale", "out_unscale", "hp_unscale",
                                    "e_scale", "minus_e_scale", "s2_scale", "s2_unscale"))
        beta_col = sb("beta_col", [P, 1])
        beta_eye = sb("beta_eye", [P, P])
        b3_col = sb("b3_col", [P, 1])

        x0 = [sb(f"x0_{p}", [P, GB, D]) for p in range(2)]
        x1 = [sb(f"x1_{p}", [P, GB, D]) for p in range(2)]
        x1_bias = [sb(f"x1_bias{p}", [P, GB, D]) for p in range(2)]
        x2 = [sb(f"x2_{p}", [P, GB, D]) for p in range(2)]
        x3 = [sb(f"x3_{p}", [P, GB, D]) for p in range(2)]
        xhat0 = sb("xhat0", [P, GB, D])
        xhat1 = sb("xhat1", [P, GB, D])
        xhat2 = sb("xhat2", [P, GB, D])
        h3 = sb("h3", [P, GB, D])
        stats = [sb(f"stats{n}", [P, GB, 6]) for n in range(4)]
        mv = [sb(f"mv{n}", [P, GB, 2]) for n in range(4)]
        veps = [sb(f"veps{n}", [P, GB]) for n in range(4)]
        negmean = [sb(f"negmean{n}", [P, GB]) for n in range(4)]
        rstd = [sb(f"rstd{n}", [P, GB]) for n in range(4)]
        shift = [sb(f"shift{n}", [P, GB]) for n in range(4)]
        hT0, hT1, hT2 = (pair(n, [P, C, COLS]) for n in ("hT0", "hT1", "hT2"))
        t0 = pair("t0", [P, C, COLS])
        relT = sb("relT", [P, COLS])
        relsq = sb("relsq", [P, COLS])
        normsq = sb("normsq", [P, GB])
        rnorm = sb("rnorm", [P, GB])
        v0 = sb("v0", [P, GB, D])
        qT = [sb(f"qT{p}", [P, C, COLS]) for p in range(2)]
        kT = sb("kT", [P, C, COLS])
        k_wide = [sb(f"k_wide{p}", [P, C, GB, HQ, N]) for p in range(2)]
        v1 = [sb(f"v1_{p}", [P, GB, D]) for p in range(2)]
        scores1 = sb("scores1", [P, 2, HQ, N])
        negmax = sb("negmax", [P, UNITS, HQ])
        probs = sb("probs", [P, 4, HQ, N])
        sums = sb("sums", [P, UNITS, HQ])
        rsums = sb("rsums", [P, UNITS, HQ])
        probsT = sb("probsT", [P, 2, HQ, N])
        attT1 = pair("attT1", [P, C, COLS])
        hp = sb("hp", [P, GB, D + 2])
        s2_cols = pair("s2_cols", [P, GB])
        s2_eye = pair("s2_eye", [P, GB, N])
        e_sum = sb("e_sum", [P, GB, N])
        e_leaky = sb("e_leaky", [P, GB, N])
        e_masked = sb("e_masked", [P, GB, N])
        max2, negmax2, sum2, rsum2 = (sb(n, [P, GB]) for n in ("max2", "negmax2", "sum2", "rsum2"))
        att2 = sb("att2", [P, GB, N])
        att2b = sb("att2b", [P, GB, N])
        att2T = sb("att2T", [P, GB, N])
        e_z = sb("e_z", [P, GB, D])
        maxA = sb("maxA", [P, GB])
        gain3 = sb("gain3", [P, GB])
        gain3m = sb("gain3m", [P, GB])

        def staged(parity, at, shape):
            flat = k_wide[parity][:].rearrange("p c b h n -> p (c b h n)")[:, at:at + int(np.prod(shape))]
            return flat.rearrange("p (c d) -> p c d", c=shape[0]) if len(shape) == 2 else flat

        w0q_in, w0k_in, w0v_in, w1q_in, w1k_in, w1v_in, w1o_in = (staged(1, n * C * D, [C, D]) for n in range(7))
        w2_in = staged(0, 0, [C, D + 2])
        at = C * (D + 2)
        a_rows, wa_junk, one_minus_adj, bo_rows = (staged(0, at + k * D, [n * D]) for k, n in
                                                   ((0, 2), (2, 1), (3, 1), (4, 1)))
        bv_wide = staged(0, at + 5 * D, [C, P])

        S = bank("S", UNITS)
        O = bank("O", 2)
        PT = bank("PT", UNITS)
        PV = bank("PV", C)
        R1 = [bank(f"R1{n}", 4) for n in range(2)]
        R0 = bank("R0", 10)
        R2 = bank("R2", 12)

        first_weights_loaded = sem("first_weights_loaded")
        weights_loaded = sem("weights_loaded")
        const_pool = sem("const_pool")
        const_dve = sem("const_dve")
        waits_taken = sem("waits_taken")
        const_pe = sem("const_pe")
        const_act = sem("const_act")
        x0_loaded = [sem(f"x0_loaded{p}") for p in range(2)]
        stored = [sem(f"stored{p}") for p in range(2)]
        stats_done = [counter(f"stats_done{n}", GB) for n in range(4)]
        mv_done = [counter(f"mv_done{n}", GB) for n in range(4)]
        ln_small = [counter(f"ln_small{n}", 4 if n == 3 else 3) for n in range(4)]
        xhat0_ready = counter("xhat0_ready", GB)
        hT0_high = counter("hT0_high", C)
        t0_high = counter("t0_high", C)
        hT1_high = counter("hT1_high", C)
        hT2_high = counter("hT2_high", C)
        attT1_high = counter("attT1_high", C)
        xhat1_ready = counter("xhat1_ready", GB)
        xhat2_ready = counter("xhat2_ready", GB)
        h3_ready = counter("h3_ready", GB)
        relsq_ready = counter("relsq_ready", 1)
        rnorm_ready = counter("rnorm_ready", 1)
        x1_bias_ready = counter("x1_bias_ready", 1)
        k_wide_ready = counter("k_wide_ready", C)
        exps_ready = counter("exps_ready", UNITS)
        rsums_ready = counter("rsums_ready", UNITS)
        probs_ready = counter("probs_ready", UNITS)
        leaky_ready = counter("leaky_ready", 1)
        max2_ready = counter("max2_ready", 2)
        s2_ready = counter("s2_ready", 3)
        exp2_ready = counter("exp2_ready", 1)
        rsum2_ready = counter("rsum2_ready", 1)
        att2_ready = counter("att2_ready", 1)
        e_z_ready = counter("e_z_ready", 2)
        x3_ready = counter("x3_ready", 2)
        gain3_ready = counter("gain3_ready", 2)
        x4_ready = counter("x4_ready", GB)

        x_groups = x.rearrange("(g b) n d -> g n b d", b=GB)
        out_groups = out.rearrange("(g b) n d -> g n b d", b=GB)

        def rows(w):
            return w.rearrange("(c p) n -> p c n", p=P)

        def chunk_columns(tile, b):
            return [(tile[:, c:c + 1], b[c * P:(c + 1) * P].rearrange("(p o) -> p o", o=1)) for c in range(C)]

        def wide(b):
            return b.rearrange("(o n) -> o n", o=1).to_broadcast([P, b.shape[0]])

        WEIGHTS = [
            (adj_sb[:], adj), (w1q_in, rows(w1q)), (w1k_in, rows(w1k)), (w1v_in, rows(w1v)), (w1o_in, rows(w1o)),
            *chunk_columns(bq_cols, b1q), *chunk_columns(bk_cols, b1k), *chunk_columns(bv_cols, b1v),
            (bo_rows, wide(b1o)), (w2_in[:, :, 0:D], rows(w2)),
            (a_rows, wide(a2.rearrange("f o -> (f o)"))), (beta_col[:], wide(beta2)),
            (b3_col[:], b3.rearrange("(p o) -> p o", o=1)),
        ]
        ALL_WEIGHTS = 16 * len(WEIGHTS)
        FIRST_WEIGHTS = [(w0q_in, rows(w0q)), (w0k_in, rows(w0k)), (w0v_in, rows(w0v))]

        def column(tile, name):
            return tile[:, SCALED.index(name):SCALED.index(name) + 1]

        def part_of(parts, value, name):
            return [part[:] for part in parts], value, name

        FIRST_SPLITS = [part_of(A0, R0.tensor[:].rearrange("p (c d) -> p c d", c=C), "A0"),
                        part_of(w0vT, R2.tensor[:].rearrange("p (c d) -> p c d", c=C), "w0v")]
        LATER_SPLITS = [part_of(w1k_sb, w1k_in, "w1k"), part_of(w1q_sb, w1q_in, "w1q"),
                        part_of(w1v_sb, w1v_in, "w1v"), part_of(w1o_sb, w1o_in, "w1o")]
        LATER_SPLITS += [([part[:, :, columns] for part in w2_aug], w2_in[:, :, columns], name)
                         for columns, name in ((slice(0, D), "w2"), (slice(D, D + 2), "wa"))]

        def apart(engine):
            engine.sem_inc(waits_taken, 1)

        def for_group(step):
            def run(g, n):
                if g.exists():
                    step(g, n)
            return run

        def iterations(engine, iteration):
            for i in range(STEADY.start):
                iteration(Group(0, i))
            assert STEADY.start % 2 == 0 and len(STEADY) % 2 == 0
            with engine.Fori(STEADY.start // 2, STEADY.stop // 2) as half:
                iteration(Group(half, 0))
                iteration(Group(half, 1))
            for i in range(STEADY.stop, ITERS):
                iteration(Group(0, i))

        block = ctx.enter_context(nc.Block())

        @block.sync
        def _(sp):
            def load(g):
                if counts(R0.drained.at(g.ahead(-2), 10)):
                    sp.wait_ge(R0.drained.sem, R0.drained.at(g.ahead(-2), 10))
                sp.dma_start(x0[g.parity][:], x_groups[g.index()]).then_inc(x0_loaded[g.parity], 16)

            def store(g):
                sp.wait_ge(x4_ready.sem, x4_ready.at(g, GB))
                sp.dma_start(out_groups[g.index()], x3[g.parity][:]).then_inc(stored[g.parity], 16)

            load(Group(0, 0))
            for dst, src in FIRST_WEIGHTS:
                sp.dma_start(dst, src).then_inc(first_weights_loaded, 16)
            for dst, src in WEIGHTS:
                sp.dma_start(dst, src).then_inc(weights_loaded, 16)

            def iteration(i):
                g = i.ahead(1)
                if g.exists():
                    load(g)
                g = i.ahead(-LAST)
                if g.exists():
                    store(g)

            for i in range(STEADY.start):
                iteration(Group(0, i))
            with sp.Fori(STEADY.start // 2, STEADY.stop // 2 - 1) as half:
                iteration(Group(half, 0))
                iteration(Group(half, 1))
            for i in range(STEADY.stop - 2, ITERS):
                iteration(Group(0, i))
            for p in range(2):
                sp.wait_ge(stored[p], 16 * (NG // 2))

        @block.tensor
        def _(pe):
            mm, transpose = nc.tensor.matmul, nc.tensor.transpose

            pe.wait_ge(first_weights_loaded, 16 * len(FIRST_WEIGHTS))
            pe.wait_ge(const_pool, 2)
            for c in range(C):
                for k in range(C):
                    last = mm(R0.tensor[:, c * D:(c + 1) * D], w0k_in[:, k, c * P:(c + 1) * P], w0q_in[:, k, :],
                              start=(k == 0), stop=(k == C - 1))
            last.then_inc(const_pe, 1)
            for c in range(C):
                for k in range(C):
                    last = transpose(R2.tensor[:, c * D + k * P:c * D + (k + 1) * P],
                                     w0v_in[:, k, c * P:(c + 1) * P], ident[:])
            last.then_inc(const_pe, 1)
            pe.wait_ge(weights_loaded, ALL_WEIGHTS)
            transpose(R1[0].tensor[:, 0:P], adj_sb[:], ident[:]).then_inc(const_pe, 1)
            pe.wait_ge(const_dve, CONST_BV)
            for c in range(C):
                last = mm(R1[1].tensor[:, 0:D], bv_wide[:, c, :], w1o_in[:, c, :], start=(c == 0), stop=(c == C - 1))
            last.then_inc(const_pe, 1)
            pe.wait_ge(const_act, len(SCALED))
            mm(S.tensor[:, 0:len(SCALED)], ones[:], w_squares[:], start=True, stop=True).then_inc(const_pe, 1)
            pe.wait_ge(const_dve, CONST_FIRST)
            pe.wait_ge(const_pool, CONST_POOL)

            def fill(bank, g, k):
                if counts(bank.drained.at(g, k)):
                    pe.wait_ge(bank.drained.sem, bank.drained.at(g, k))

            def turn(bank, g, k, src, c):
                fill(bank, g, k)
                for b in range(GB):
                    last = transpose(bank.tensor[:, b * N:(b + 1) * N], src[:, b, c * P:(c + 1) * P], ident[:])
                last.then_inc(bank.filled.sem, 1)

            def product(dst, lhsT, rhs):
                steps = [(c, i, j) for c in range(C) for i, j in PASSES]
                for n, (c, i, j) in enumerate(steps):
                    last = mm(dst, lhsT(i, c), rhs(j, c), start=(n == 0), stop=(n == len(steps) - 1))
                return last

            def project_T(bank, g, k, w, hT, m):
                fill(bank, g, k)
                last = product(bank.tensor[:], lambda i, c: w[i][:, c, m * P:(m + 1) * P], lambda j, c: hT[j][:, c, :])
                last.then_inc(bank.filled.sem, 1)

            def project(bank, g, k, hT, w, half):
                fill(bank, g, k)
                for n, b in enumerate((2 * half, 2 * half + 1)):
                    last = product(bank.tensor[:, n * D:(n + 1) * D], lambda i, c: hT[i][:, c, b * N:(b + 1) * N],
                                   lambda j, c: w[j][:, c, :])
                last.then_inc(bank.filled.sem, 1)

            @for_group
            def layer0(g, step):
                if step < 2:
                    pe.wait_ge(xhat0_ready.sem, xhat0_ready.at(g, GB))
                    turn(R0, g, step, xhat0, step)
                elif step < 4:
                    project_T(R0, g, step, A0, hT0, step - 2)
                elif step == 4:
                    fill(R0, g, 4)
                    for b in range(GB):
                        s = slice(b * N, (b + 1) * N)
                        last = product(R0.tensor[:, s], lambda i, c: t0[i][:, c, s], lambda j, c: hT0[j][:, c, s])
                    last.then_inc(R0.filled.sem, 1)
                elif step < 7:
                    project(R0, g, step, hT0, w0vT, step - 5)
                elif step == 7:
                    fill(R0, g, 7)
                    pe.wait_ge(relsq_ready.sem, relsq_ready.at(g, 1))
                    for b in range(GB):
                        s = slice(b * N, (b + 1) * N)
                        last = mm(R0.tensor[:, s], relsq[:, s], ones[:], start=True, stop=True)
                    last.then_inc(R0.filled.sem, 1)
                else:
                    fill(R0, g, step)
                    for n, b in enumerate((2 * (step - 8), 2 * (step - 8) + 1)):
                        last = mm(R0.tensor[:, n * D:(n + 1) * D], relT[:, b * N:(b + 1) * N], v0[:, b, :],
                                  start=True, stop=True)
                    last.then_inc(R0.filled.sem, 1)

            @for_group
            def turn1(g, c):
                pe.wait_ge(xhat1_ready.sem, xhat1_ready.at(g, GB))
                turn(R1[c], g, 0, xhat1, c)

            def both_hT1(g):
                for n in range(2):
                    pe.wait_ge(R1[n].drained.sem, R1[n].drained.at(g, 1))

            @for_group
            def keys(g, m):
                if g.first():
                    pe.wait_ge(const_dve, CONST_DVE)
                both_hT1(g)
                project_T(R1[m], g, 1, w1k_sb, hT1, m)

            @for_group
            def queries(g, m):
                project_T(R1[m], g, 2, w1q_sb, hT1, m)

            @for_group
            def values(g, half):
                project(R1[half], g, 3, hT1, w1v_sb, half)

            @for_group
            def scores(g, u):
                m, b = divmod(u, GB)
                fill(S, g, u)
                pe.wait_ge(k_wide_ready.sem, k_wide_ready.at(g, m + 1))
                pe.wait_ge(R1[m].drained.sem, R1[m].drained.at(g, 3))
                last = mm(S.tensor[:], qT[g.parity][:, m, b * N:(b + 1) * N],
                          k_wide[g.parity][:, m, b, :, :].rearrange("p h n -> p (h n)"), start=True, stop=True)
                last.then_inc(S.filled.sem, 1)

            @for_group
            def turn_probs(g, u):
                fill(PT, g, u)
                pe.wait_ge(probs_ready.sem, probs_ready.at(g, u + 1))
                for h in range(HQ):
                    last = transpose(PT.tensor[:, h * N:(h + 1) * N], probs[:, u % 4, h, :], ident[:])
                last.then_inc(PT.filled.sem, 1)

            @for_group
            def weigh_values(g, u):
                m, b = divmod(u, GB)
                if b == 0:
                    fill(PV, g, m)
                pe.wait_ge(PT.drained.sem, PT.drained.at(g, u + 1))
                if u == 0:
                    for n in range(2):
                        pe.wait_ge(R1[n].drained.sem, R1[n].drained.at(g, 4))
                for h in range(HQ):
                    last = mm(PV.tensor[h * HD:(h + 1) * HD, b * N:(b + 1) * N],
                              v1[g.parity][:, b, m * P + h * HD:m * P + (h + 1) * HD], probsT[:, u % 2, h, :],
                              start=True, stop=True, tile_position=(0, h * HD))
                if b == GB - 1:
                    last.then_inc(PV.filled.sem, 1)

            @for_group
            def project_out(g, half):
                pe.wait_ge(PV.drained.sem, PV.drained.at(g, C))
                project(O, g, half, attT1, w1o_sb, half)

            @for_group
            def layer2(g, step):
                if step < 2:
                    pe.wait_ge(xhat2_ready.sem, xhat2_ready.at(g, GB))
                    turn(R2, g, step, xhat2, step)
                elif step == 6:
                    fill(R2, g, 6)
                    pe.wait_ge(s2_ready.sem, s2_ready.at(g, 3))
                    for part in range(2):
                        last = mm(R2.tensor[:], ones_half[:], s2_eye[part][:].rearrange("p b n -> p (b n)"),
                                  start=(part == 0), stop=(part == 1))
                    last.then_inc(R2.filled.sem, 1)
                elif step < 6:
                    b = step - 2
                    fill(R2, g, step)
                    last = product(R2.tensor[:, 0:D + 2], lambda i, c: hT2[i][:, c, b * N:(b + 1) * N],
                                   lambda j, c: w2_aug[j][:, c, :])
                    last.then_inc(R2.filled.sem, 1)
                elif step == 7:
                    fill(R2, g, 7)
                    pe.wait_ge(att2_ready.sem, att2_ready.at(g, 1))
                    for b in range(GB):
                        last = transpose(R2.tensor[:, b * N:(b + 1) * N], att2b[:, b, :], ident[:])
                    last.then_inc(R2.filled.sem, 1)
                else:
                    fill(R2, g, step)
                    for n, b in enumerate((2 * (step - 8), 2 * (step - 8) + 1)):
                        last = mm(R2.tensor[:, n * D:(n + 1) * D], att2T[:, b, :], hp[:, b, 0:D], start=True, stop=True)
                    last.then_inc(R2.filled.sem, 1)

            @for_group
            def layer3(g, half):
                pe.wait_ge(h3_ready.sem, h3_ready.at(g, 2 * half + 2))
                fill(R2, g, 10 + half)
                last = mm(R2.tensor[:], adj_T[:],
                          h3[:, 2 * half:2 * half + 2, :].rearrange("p b d -> p (b d)"), start=True, stop=True)
                last.then_inc(R2.filled.sem, 1)

            def iteration(i):
                g0, g1, g2, g3, g4, g5 = (i.ahead(-lag) for lag in range(LAST + 1))
                layer0(g1, 1)
                layer2(g5, 6)
                turn_probs(g4, 7)
                values(g3, 1)
                layer0(g1, 2)
                weigh_values(g4, 7)
                turn1(g2, 0)

                scores(g3, 3)
                turn_probs(g3, 0)
                layer0(g1, 3)
                turn1(g2, 1)
                project_out(g4, 0)
                weigh_values(g3, 0)

                scores(g3, 4)
                layer2(g5, 7)
                layer0(g1, 4)
                turn_probs(g3, 1)
                layer2(g5, 8)
                project_out(g4, 1)
                keys(g2, 0)
                layer2(g5, 9)
                weigh_values(g3, 1)
                layer0(g1, 5)

                scores(g3, 5)
                queries(g2, 0)
                turn_probs(g3, 2)
                layer0(g1, 6)

                scores(g3, 6)
                keys(g2, 1)
                layer3(g5, 0)
                turn_probs(g3, 3)

                scores(g3, 7)
                layer3(g5, 1)
                layer0(g1, 7)
                weigh_values(g3, 2)
                layer2(g4, 0)
                queries(g2, 1)
                turn_probs(g3, 4)
                layer2(g4, 1)
                layer0(g1, 8)
                weigh_values(g3, 3)

                scores(g2, 0)
                layer2(g4, 2)
                turn_probs(g3, 5)
                layer0(g1, 9)
                layer2(g4, 3)

                scores(g2, 1)
                weigh_values(g3, 4)
                layer2(g4, 4)
                turn_probs(g3, 6)
                layer0(g0, 0)
                layer2(g4, 5)
                weigh_values(g3, 5)
                values(g2, 0)

                scores(g2, 2)
                weigh_values(g3, 6)

            iterations(pe, iteration)

        @block.scalar
        def _(act):
            activation = nc.scalar.activation

            def copy_out(bank, g, k, dst, src=None, func=ACT.Copy, **kw):
                act.wait_ge(bank.filled.sem, bank.filled.at(g, k + 1))
                activation(dst, bank.tensor[:] if src is None else src, func, **kw)\
                    .then_inc(bank.drained.sem, 1)

            def high_out(bank, g, k, dst, ready, func, **kw):
                act.wait_ge(bank.filled.sem, bank.filled.at(g, k + 1))
                activation(dst, bank.tensor[:], func, **kw).then_inc(ready.sem, 1)

            @for_group
            def norm3(g, _):
                act.wait_ge(ln_small[3].sem, ln_small[3].at(g, 4))
                if counts(R2.filled.at(g, 0)):
                    act.wait_ge(R2.filled.sem, R2.filled.at(g, 0))
                for b in range(GB):
                    activation(h3[:, b, :], x3[g.parity][:, b, :], ACT.Relu, bias=shift[3][:, b:b + 1],
                               scale=rstd[3][:, b:b + 1]).then_inc(h3_ready.sem, 1)

            @for_group
            def layer0(g, k):
                if k < 2:
                    high_out(R0, g, k, hT0[0][:, k, :], hT0_high, ACT.Relu)
                elif k < 4:
                    if k == 2 and g.first():
                        high_parts(LATER_SPLITS)
                    high_out(R0, g, k, t0[0][:, k - 2, :], t0_high, ACT.Copy, scale=1 / T_SCALE)
                else:
                    half = k - 5
                    if g.first():
                        act.wait_ge(const_dve, CONST_DVE)
                    copy_out(R0, g, k, v0[:, 2 * half:2 * half + 2, :].rearrange("p b d -> p (b d)"),
                             scale=v0_unscale[:, 0:1])

            @for_group
            def relu_hT1(g, c):
                high_out(R1[c], g, 0, hT1[0][:, c, :], hT1_high, ACT.Relu)

            @for_group
            def queries(g, m):
                copy_out(R1[m], g, 2, qT[g.parity][:, m, :], func=ACT.Identity, bias=bq_scaled[:, m:m + 1],
                         scale=q_unscale[:, 0:1])

            @for_group
            def values(g, half):
                copy_out(R1[half], g, 3, v1[g.parity][:, 2 * half:2 * half + 2, :].rearrange("p b d -> p (b d)"),
                         scale=1 / V_SCALE)

            @for_group
            def exps(g, u):
                act.wait_ge(S.drained.sem, S.drained.at(g, u + 1))
                for h in range(HQ):
                    last = activation(probs[:, u % 4, h, :], scores1[:, u % 2, h, :], ACT.Exp, scale=-1.0,
                                      bias=negmax[:, u, h:h + 1], accum_out=sums[:, u, h:h + 1])
                last.then_inc(exps_ready.sem, 1)

            @for_group
            def probs_out(g, u):
                copy_out(PT, g, u, probsT[:, u % 2, :, :].rearrange("p h n -> p (h n)"))

            @for_group
            def attention_out(g, m):
                high_out(PV, g, m, attT1[0][:, m, :], attT1_high, ACT.Copy)

            @for_group
            def layer2(g, k):
                if k < 2:
                    high_out(R2, g, k, hT2[0][:, k, :], hT2_high, ACT.Relu)
                elif k < 6:
                    copy_out(R2, g, k, hp[:, k - 2, :], src=R2.tensor[:, 0:D + 2], scale=hp_unscale[:, 0:1])
                elif k == 6:
                    act.wait_ge(R2.filled.sem, R2.filled.at(g, 7))
                    act.wait_ge(R2.drained.sem, R2.drained.at(g, 6))
                    for b in range(GB):
                        last = activation(e_sum[:, b, :], R2.tensor[:, b * N:(b + 1) * N], ACT.Identity,
                                          bias=hp[:, b, D:D + 1], scale=s2_unscale[:, 0:1])
                    last.then_inc(R2.drained.sem, 1)
                elif k == 7:
                    copy_out(R2, g, 7, att2T[:].rearrange("p b n -> p (b n)"))
                else:
                    half = k - 8
                    act.wait_ge(R2.filled.sem, R2.filled.at(g, k + 1))
                    activation(e_z[:, 2 * half:2 * half + 2, :].rearrange("p b d -> p (b d)"), R2.tensor[:], ACT.Exp)\
                        .then_inc(e_z_ready.sem, 1)

            @for_group
            def softmax2(g, _):
                act.wait_ge(max2_ready.sem, max2_ready.at(g, 2))
                for b in range(GB):
                    last = activation(att2[:, b, :], e_masked[:, b, :], ACT.Exp, bias=negmax2[:, b:b + 1],
                                      scale=e_scale[:, 0:1],
                                      accum_out=sum2[:, b:b + 1])
                last.then_inc(exp2_ready.sem, 1)

            def high_parts(splits):
                for parts, value, name in splits:
                    activation(parts[0], value, ACT.Copy, scale=column(w_scale, name)).then_inc(const_act, 1)

            act.wait_ge(weights_loaded, ALL_WEIGHTS)
            squares_junk = O.tensor[:].rearrange("p (c d) -> p c d", c=C)
            for n, (_, value, name) in enumerate(LATER_SPLITS + FIRST_SPLITS):
                if n > 0:
                    act.wait_ge(const_act, n)
                if name == "A0":
                    act.wait_ge(const_pe, 2)
                if name == "w2":
                    act.wait_ge(const_dve, CONST_WA)
                columns = value.shape[-1]
                activation(squares_junk[:, :, 0:columns], value, ACT.Square, accum_out=column(w_squares, name))\
                    .then_inc(const_act, 1)
            act.wait_ge(const_dve, CONST_SCALES)
            high_parts(FIRST_SPLITS)

            def iteration(i):
                g0, g1, g2, g3, g4, g5 = (i.ahead(-lag) for lag in range(LAST + 1))
                layer0(g1, 1)
                layer2(g5, 6)
                values(g3, 0)
                layer0(g1, 2)
                relu_hT1(g2, 0)
                attention_out(g4, 1)
                softmax2(g5, 0)
                probs_out(g3, 0)
                layer0(g1, 3)
                relu_hT1(g2, 1)

                exps(g3, 2)
                layer2(g5, 7)
                layer2(g5, 8)
                layer2(g5, 9)

                exps(g3, 3)
                layer0(g1, 5)

                exps(g3, 4)
                probs_out(g3, 2)
                layer0(g1, 6)
                norm3(g5, 0)

                exps(g3, 5)
                queries(g2, 0)

                exps(g3, 6)
                layer2(g4, 0)

                exps(g3, 7)
                layer2(g4, 1)
                probs_out(g3, 4)
                attention_out(g3, 0)
                queries(g2, 1)
                layer2(g4, 2)
                layer2(g4, 3)

                exps(g2, 0)
                layer2(g4, 4)
                probs_out(g3, 6)
                layer0(g0, 0)
                layer2(g4, 5)

                exps(g2, 1)

            iterations(act, iteration)

        @block.vector
        def _(dve):
            v = nc.vector
            built = [0]

            def constant(instruction):
                instruction.then_inc(const_dve, 1)
                built[0] += 1
                dve.wait_ge(const_dve, built[0])

            def power_of_two(dst, src):
                constant(v.tensor_scalar(w_span[:], src, 2.0 ** 23 + 1, None, ALU.mult))
                constant(v.tensor_tensor(w_part[:], w_span[:], src, ALU.subtract))
                constant(v.tensor_tensor(dst, w_span[:], w_part[:], ALU.subtract))

            def factors():
                constant(v.reciprocal(w_unscale[:], w_scale[:]))
                power_of_two(w_unscale[:], w_unscale[:])
                constant(v.tensor_scalar(v0_unscale[:], column(w_unscale, "w0v"), 1 / H_SCALE, None, ALU.mult))
                constant(v.tensor_scalar(q_unscale[:], column(w_unscale, "w1q"), HD ** -0.5 / H_SCALE, None, ALU.mult))
                constant(v.tensor_scalar(k_unscale[:], column(w_unscale, "w1k"), 1 / H_SCALE, None, ALU.mult))
                constant(v.tensor_tensor(out_unscale[:], column(w_unscale, "w1v"), column(w_unscale, "w1o"), ALU.mult))
                constant(v.tensor_scalar(hp_unscale[:], column(w_unscale, "w2"), 1 / H_SCALE, None, ALU.mult))
                constant(v.tensor_tensor(e_scale[:], column(w_unscale, "wa"), column(w_scale, "w2"), ALU.mult))
                constant(v.tensor_scalar(minus_e_scale[:], e_scale[:], -1.0, None, ALU.mult))
                constant(v.tensor_scalar(s2_scale[:], column(w_scale, "w2"), S2_SCALE / W_NORM, None, ALU.mult))
                constant(v.tensor_scalar(s2_unscale[:], column(w_unscale, "w2"), W_NORM / S2_SCALE, None, ALU.mult))

            def low_parts(splits):
                for parts, value, name in splits:
                    first = (FIRST_SPLITS + LATER_SPLITS).index((parts, value, name))
                    dve.wait_ge(const_act, len(SCALED) + first + 1)
                    constant(v.scalar_tensor_tensor(parts[1], value, column(w_scale, name), parts[0],
                                                    ALU.mult, ALU.subtract))

            def copy_out(bank, g, k, dst):
                dve.wait_ge(bank.filled.sem, bank.filled.at(g, k + 1))
                v.tensor_copy(dst, bank.tensor[:]).then_inc(bank.drained.sem, 1)

            def low_out(bank, g, k, parts, c, ready):
                dve.wait_ge(ready.sem, ready.at(g, c + 1))
                v.scalar_tensor_tensor(parts[1][:, c, :], bank.tensor[:], 0.0, parts[0][:, c, :],
                                       ALU.max, ALU.subtract).then_inc(bank.drained.sem, 1)

            def statistics(n, g, src, batches, last):
                for b in batches:
                    v.bn_stats(stats[n][:, b, :], src[:, b, :]).then_inc(stats_done[n].sem, 1)
                if last:
                    if counts(ln_small[n].at(g, 0)):
                        dve.wait_ge(ln_small[n].sem, ln_small[n].at(g, 0))
                    for b in range(GB):
                        dve.wait_ge(stats_done[n].sem, stats_done[n].at(g, b + 1))
                        apart(dve)
                        v.bn_aggr(mv[n][:, b, :], stats[n][:, b, :]).then_inc(mv_done[n].sem, 1)

            def statistics0(g):
                dve.wait_ge(x0_loaded[g.parity], g.pair_times(16, 16))
                statistics(0, g, x0[g.parity], range(GB), True)

            @for_group
            def norm0(g, _):
                if not g.first():
                    statistics0(g)

            @for_group
            def layer0(g, k):
                if k < 2:
                    low_out(R0, g, k, hT0, k, hT0_high)
                elif k < 4:
                    if k == 2 and g.first():
                        factors()
                    dve.wait_ge(t0_high.sem, t0_high.at(g, k - 1))
                    v.scalar_tensor_tensor(t0[1][:, k - 2, :], R0.tensor[:], 1 / T_SCALE, t0[0][:, k - 2, :],
                                           ALU.mult, ALU.subtract).then_inc(R0.drained.sem, 1)
                elif k == 4:
                    if g.first():
                        low_parts(LATER_SPLITS)
                        assert built[0] == CONST_DVE
                    dve.wait_ge(R0.filled.sem, R0.filled.at(g, 5))
                    v.tensor_tensor(relT[:].rearrange("p (b n) -> p b n", b=GB),
                                    R0.tensor[:].rearrange("p (b n) -> p b n", b=GB),
                                    adj_sb[:].unsqueeze(1).to_broadcast([P, GB, N]), ALU.mult)\
                        .then_inc(R0.drained.sem, 1)
                elif k == 7:
                    dve.wait_ge(R0.filled.sem, R0.filled.at(g, 8))
                    if counts(rnorm_ready.at(g, 0)):
                        dve.wait_ge(rnorm_ready.sem, rnorm_ready.at(g, 0))
                    v.tensor_copy(normsq[:], R0.tensor[:, 0:COLS:N]).then_inc(R0.drained.sem, 1)
                else:
                    half = k - 8
                    dve.wait_ge(R0.filled.sem, R0.filled.at(g, k + 1))
                    if half == 0:
                        dve.wait_ge(rnorm_ready.sem, rnorm_ready.at(g, 1))
                        if counts(xhat1_ready.at(g, 0)):
                            dve.wait_ge(xhat1_ready.sem, xhat1_ready.at(g, 0))
                        if counts(x1_bias_ready.at(g.ahead(-1), 0)):
                            dve.wait_ge(x1_bias_ready.sem, x1_bias_ready.at(g.ahead(-1), 0))
                    for n, b in enumerate((2 * half, 2 * half + 1)):
                        last = v.scalar_tensor_tensor(x1[g.parity][:, b, :], R0.tensor[:, n * D:(n + 1) * D],
                                                      rnorm[:, b:b + 1], x0[g.parity][:, b, :], ALU.mult, ALU.add)
                    last.then_inc(R0.drained.sem, 1)

            @for_group
            def norm1(g, _):
                dve.wait_ge(R0.drained.sem, R0.drained.at(g, 10))
                statistics(1, g, x1[g.parity], range(GB), True)

            @for_group
            def relu_hT1(g, c):
                low_out(R1[c], g, 0, hT1, c, hT1_high)

            @for_group
            def keys(g, m):
                dve.wait_ge(R1[m].filled.sem, R1[m].filled.at(g, 2))
                if counts(k_wide_ready.at(g, 0)):
                    dve.wait_ge(k_wide_ready.sem, k_wide_ready.at(g, 0))
                v.tensor_scalar(kT[:, m, :], R1[m].tensor[:], k_unscale[:, 0:1], bk_cols[:, m:m + 1], ALU.mult, ALU.add)\
                    .then_inc(R1[m].drained.sem, 1)

            @for_group
            def values(g, half):
                dve.wait_ge(R1[half].filled.sem, R1[half].filled.at(g, 4))
                v.tensor_scalar(v1[g.parity][:, 2 * half:2 * half + 2, :].rearrange("p b d -> p (b d)"),
                                R1[half].tensor[:], 1 / V_SCALE, None, ALU.mult).then_inc(R1[half].drained.sem, 1)

            @for_group
            def maxima(g, u):
                dve.wait_ge(S.filled.sem, S.filled.at(g, u + 1))
                if counts(exps_ready.at(g.ahead(-1), UNITS + u - 1)):
                    dve.wait_ge(exps_ready.sem, exps_ready.at(g.ahead(-1), UNITS + u - 1))
                apart(dve)
                for h in range(HQ):
                    last = v.tensor_tensor_reduce(scores1[:, u % 2, h, :], S.tensor[:, h * N:(h + 1) * N], mask1[:],
                                                  -1.0, BIG, ALU.add, ALU.min, negmax[:, u, h:h + 1])
                last.then_inc(S.drained.sem, 1)

            @for_group
            def invert_sums(g, u):
                dve.wait_ge(exps_ready.sem, exps_ready.at(g, u + 1))
                if counts(probs_ready.at(g.ahead(-1), u + 1)):
                    dve.wait_ge(probs_ready.sem, probs_ready.at(g.ahead(-1), u + 1))
                v.reciprocal(rsums[:, u, :], sums[:, u, :]).then_inc(rsums_ready.sem, 1)

            @for_group
            def probs_out(g, u):
                copy_out(PT, g, u, probsT[:, u % 2, :, :].rearrange("p h n -> p (h n)"))

            @for_group
            def attention_out(g, m):
                dve.wait_ge(attT1_high.sem, attT1_high.at(g, m + 1))
                v.tensor_tensor(attT1[1][:, m, :], PV.tensor[:], attT1[0][:, m, :], ALU.subtract)\
                    .then_inc(PV.drained.sem, 1)

            @for_group
            def residual1(g, half):
                dve.wait_ge(O.filled.sem, O.filled.at(g, half + 1))
                dve.wait_ge(x1_bias_ready.sem, x1_bias_ready.at(g, 1))
                if half == 0:
                    if counts(xhat2_ready.at(g, 0)):
                        dve.wait_ge(xhat2_ready.sem, xhat2_ready.at(g, 0))
                rows_ = slice(2 * half, 2 * half + 2)
                v.scalar_tensor_tensor(x2[g.parity][:, rows_, :].rearrange("p b d -> p (b d)"), O.tensor[:],
                                       out_unscale[:, 0:1],
                                       x1_bias[g.parity][:, rows_, :].rearrange("p b d -> p (b d)"), ALU.mult, ALU.add)\
                    .then_inc(O.drained.sem, 1)
                dve.wait_ge(O.drained.sem, O.drained.at(g, half + 1))
                statistics(2, g, x2[g.parity], (2 * half, 2 * half + 1), half == 1)

            @for_group
            def layer2(g, k):
                if k < 2:
                    low_out(R2, g, k, hT2, k, hT2_high)
                else:
                    dve.wait_ge(R2.drained.sem, R2.drained.at(g, 7))
                    v.scalar_tensor_tensor(e_leaky[:], e_sum[:], ALPHA, e_sum[:], ALU.mult, ALU.max)\
                        .then_inc(leaky_ready.sem, 1)
                    dve.wait_ge(leaky_ready.sem, leaky_ready.at(g, 1))
                    if counts(exp2_ready.at(g, 0)):
                        dve.wait_ge(exp2_ready.sem, exp2_ready.at(g, 0))
                    apart(dve)
                    for b in range(GB):
                        last = v.tensor_tensor_reduce(e_masked[:, b, :], e_leaky[:, b, :], adj_sb[:], 1.0, -3.4e38,
                                                      ALU.mult, ALU.max, max2[:, b:b + 1])
                    last.then_inc(max2_ready.sem, 1)
                    dve.wait_ge(max2_ready.sem, max2_ready.at(g, 1))
                    v.tensor_scalar(negmax2[:], max2[:], minus_e_scale[:, 0:1], None, ALU.mult).then_inc(max2_ready.sem, 1)

            @for_group
            def spread_s2(g, _):
                dve.wait_ge(R2.drained.sem, R2.drained.at(g, 6))
                if counts(R2.filled.at(g.ahead(-1), 7)):
                    dve.wait_ge(R2.filled.sem, R2.filled.at(g.ahead(-1), 7))
                v.tensor_scalar(s2_cols[0][:], hp[:, :, D + 1], s2_scale[:, 0:1], None, ALU.mult)\
                    .then_inc(s2_ready.sem, 1)
                dve.wait_ge(s2_ready.sem, s2_ready.at(g, 1))
                v.scalar_tensor_tensor(s2_cols[1][:], hp[:, :, D + 1], s2_scale[:, 0:1], s2_cols[0][:],
                                       ALU.mult, ALU.subtract).then_inc(s2_ready.sem, 1)
                dve.wait_ge(s2_ready.sem, s2_ready.at(g, 2))
                for part in range(2):
                    last = v.tensor_tensor(s2_eye[part][:], ident_half[:].unsqueeze(1).to_broadcast([P, GB, N]),
                                           s2_cols[part][:].unsqueeze(2).to_broadcast([P, GB, N]), ALU.mult)
                last.then_inc(s2_ready.sem, 1)

            @for_group
            def weights2(g, _):
                dve.wait_ge(exp2_ready.sem, exp2_ready.at(g, 1))
                v.reciprocal(rsum2[:], sum2[:]).then_inc(rsum2_ready.sem, 1)
                dve.wait_ge(rsum2_ready.sem, rsum2_ready.at(g, 1))
                for b in range(GB):
                    last = v.scalar_tensor_tensor(att2b[:, b, :], att2[:, b, :], rsum2[:, b:b + 1], beta_eye[:],
                                                  ALU.mult, ALU.add)
                last.then_inc(att2_ready.sem, 1)

            @for_group
            def elu(g, half):
                rows_ = slice(2 * half, 2 * half + 2)
                flat = lambda t: t[:, rows_, :].rearrange("p b d -> p (b d)")
                dve.wait_ge(e_z_ready.sem, e_z_ready.at(g, half + 1))
                last = v.scalar_tensor_tensor(flat(x2[g.parity]), R2.tensor[:], 0.0, flat(x2[g.parity]),
                                              ALU.max, ALU.add)
                last.then_inc(R2.drained.sem, 1)
                if counts(R2.drained.at(g, 9 + half)):
                    dve.wait_ge(R2.drained.sem, R2.drained.at(g, 9 + half))
                if half == 0:
                    if counts(g.pair_times(16)):
                        dve.wait_ge(stored[g.parity], g.pair_times(16))
                v.scalar_tensor_tensor(flat(x3[g.parity]), flat(e_z), 1.0, flat(x2[g.parity]), ALU.min, ALU.add)\
                    .then_inc(x3_ready.sem, 1)
                dve.wait_ge(x3_ready.sem, x3_ready.at(g, half + 1))
                statistics(3, g, x3[g.parity], (2 * half, 2 * half + 1), half == 1)

            @for_group
            def layer3(g, half):
                if counts(R2.filled.at(g, 11 + half)):
                    dve.wait_ge(R2.filled.sem, R2.filled.at(g, 11 + half))
                v.tensor_reduce(maxA[:, 2 * half:2 * half + 2], R2.tensor[:].rearrange("p (b n) -> p b n", b=2),
                                AX.X, ALU.max).then_inc(R2.drained.sem, 1)
                if half == 1:
                    dve.wait_ge(R2.drained.sem, R2.drained.at(g, 12))
                    v.tensor_scalar(gain3[:], maxA[:], b3_col[:, 0:1], 0.0, ALU.add, ALU.max)\
                        .then_inc(gain3_ready.sem, 1)
                    dve.wait_ge(gain3_ready.sem, gain3_ready.at(g, 1))
                    if counts(x4_ready.at(g, 0)):
                        dve.wait_ge(x4_ready.sem, x4_ready.at(g, 0))
                    v.tensor_scalar(gain3m[:], gain3[:], -1.0, None, ALU.add).then_inc(gain3_ready.sem, 1)

            statistics0(Group(0, 0))
            dve.wait_ge(weights_loaded, ALL_WEIGHTS)
            dve.wait_ge(const_pool, 3)
            for c in range(C):
                constant(v.tensor_scalar(bv_wide[:, c, :], ones[:], bv_cols[:, c:c + 1], None, ALU.mult))
            assert built[0] == CONST_BV
            constant(v.tensor_scalar(one_minus_adj[:, 0:P], adj_sb[:], -1.0, 1.0, ALU.mult, ALU.add))
            constant(v.tensor_scalar(mask1[:], one_minus_adj[:, 0:P], -1e9, None, ALU.mult))
            constant(v.tensor_scalar(bq_scaled[:], bq_cols[:], HD ** -0.5, None, ALU.mult))
            for c in range(C):
                for half in range(2):
                    constant(v.tensor_tensor_reduce(wa_junk, w2_in[:, c, 0:D], a_rows[:, half * D:(half + 1) * D],
                                                    1.0, 0.0, ALU.mult, ALU.add, w2_in[:, c, D + half:D + half + 1]))
            assert built[0] == CONST_WA
            constant(v.tensor_copy(ident_half[:], ident[:]))
            constant(v.tensor_copy(ones_half[:], ones[:]))
            constant(v.tensor_scalar(beta_eye[:], ident[:], beta_col[:, 0:1], None, ALU.mult))
            dve.wait_ge(const_pe, 3)
            constant(v.tensor_copy(adj_T[:], R1[0].tensor[:, 0:P]))
            dve.wait_ge(const_pe, 4)
            constant(v.tensor_tensor(bias1[:], R1[1].tensor[:, 0:D], bo_rows, ALU.add))
            dve.wait_ge(const_pe, 5)
            constant(v.tensor_scalar(w_total[:], S.tensor[:, 0:len(SCALED)], SQUARES_MIN, SQUARES_MAX, ALU.max, ALU.min))
            assert built[0] == CONST_TOTAL
            dve.wait_ge(const_pool, CONST_POOL + 1)
            power_of_two(w_power[:], w_rnorm[:])
            constant(v.tensor_scalar(w_scale[:], w_power[:], W_NORM, None, ALU.mult))
            assert built[0] == CONST_SCALES
            low_parts(FIRST_SPLITS)
            assert built[0] == CONST_FIRST

            def iteration(i):
                g0, g1, g2, g3, g4, g5 = (i.ahead(-lag) for lag in range(LAST + 1))
                invert_sums(g3, 0)
                invert_sums(g3, 1)

                maxima(g3, 2)
                layer0(g1, 1)
                probs_out(g4, 7)
                layer2(g5, 7)
                layer0(g1, 2)
                values(g3, 1)
                attention_out(g4, 1)
                relu_hT1(g2, 0)

                maxima(g3, 3)
                weights2(g5, 0)
                layer0(g1, 3)
                residual1(g4, 0)
                relu_hT1(g2, 1)
                layer0(g1, 4)
                probs_out(g3, 1)

                maxima(g3, 4)
                invert_sums(g3, 2)
                elu(g5, 0)
                keys(g2, 0)
                elu(g5, 1)
                invert_sums(g3, 3)

                maxima(g3, 5)
                residual1(g4, 1)
                invert_sums(g3, 4)

                maxima(g3, 6)
                keys(g2, 1)
                layer3(g5, 0)

                maxima(g3, 7)
                layer3(g5, 1)
                layer0(g1, 7)
                invert_sums(g3, 5)
                invert_sums(g3, 6)
                probs_out(g3, 3)
                layer2(g4, 0)
                norm0(g0, 0)
                layer2(g4, 1)
                invert_sums(g3, 7)
                layer0(g1, 8)
                attention_out(g3, 0)

                maxima(g2, 0)
                probs_out(g3, 5)
                layer0(g1, 9)

                maxima(g2, 1)
                norm1(g1, 0)
                layer0(g0, 0)
                spread_s2(g4, 0)

            iterations(dve, iteration)

        @block.gpsimd
        def _(pool):
            p = nc.gpsimd
            p.memset(ident[:], 0.0).then_inc(const_pool, 1)
            pool.wait_ge(const_pool, 1)
            p.affine_select(out=ident[:], in_=ident[:], compare_op=ALU.not_equal, fill=1.0, base=0,
                            pattern=[[-1, P]], channel_multiplier=1).then_inc(const_pool, 1)
            p.memset(ones[:], 1.0).then_inc(const_pool, 1)
            p.memset(minus_half[:], -0.5).then_inc(const_pool, 1)
            p.memset(head_rows[:], 1.0).then_inc(const_pool, 1)
            for base, sign in ((0, 1), (HD - 1, -1)):
                pool.wait_ge(const_pool, 5 if sign > 0 else 6)
                p.affine_select(out=head_rows[:], in_=head_rows[:], compare_op=ALU.is_ge, fill=0.0, base=base,
                                pattern=[[-sign * HD, HQ]], channel_multiplier=sign).then_inc(const_pool, 1)
            pool.wait_ge(const_pool, CONST_POOL)
            def small(n, g):
                pool.wait_ge(mv_done[n].sem, mv_done[n].at(g, GB))
                apart(pool)
                p.tensor_scalar(veps[n][:], mv[n][:, :, 1], EPS, 1.0 if n == 3 else H_SCALE ** -2, ALU.add, ALU.mult)\
                    .then_inc(ln_small[n].sem, 1)
                p.tensor_scalar(negmean[n][:], mv[n][:, :, 0], -1.0, 0.0, ALU.mult, ALU.add)\
                    .then_inc(ln_small[n].sem, 1)
                pool.wait_ge(ln_small[n].sem, ln_small[n].at(g, 1))
                if n == 3:
                    if counts(h3_ready.at(g, 0)):
                        pool.wait_ge(h3_ready.sem, h3_ready.at(g, 0))
                p.tensor_tensor(rstd[n][:], veps[n][:], minus_half[:], ALU.pow).then_inc(ln_small[n].sem, 1)
                pool.wait_ge(ln_small[n].sem, ln_small[n].at(g, 3))
                if n == 3:
                    p.tensor_tensor(shift[n][:], negmean[n][:], rstd[n][:], ALU.mult).then_inc(ln_small[n].sem, 1)

            def normalise(n, g, dst, src, ready):
                small(n, g)
                apart(pool)
                for b in range(GB):
                    p.tensor_scalar(dst[:, b, :], src[:, b, :], negmean[n][:, b:b + 1], rstd[n][:, b:b + 1],
                                    ALU.add, ALU.mult).then_inc(ready.sem, 1)

            def normalise0(g):
                if counts(R0.filled.at(g.ahead(-1), 2)):
                    pool.wait_ge(R0.filled.sem, R0.filled.at(g.ahead(-1), 2))
                normalise(0, g, xhat0, x0[g.parity], xhat0_ready)

            @for_group
            def norm0(g, _):
                if not g.first():
                    normalise0(g)

            @for_group
            def norm1(g, _):
                if counts(R1[1].filled.at(g.ahead(-1), 1)):
                    pool.wait_ge(R1[1].filled.sem, R1[1].filled.at(g.ahead(-1), 1))
                normalise(1, g, xhat1, x1[g.parity], xhat1_ready)

            @for_group
            def norm2(g, _):
                if counts(R2.filled.at(g.ahead(-1), 2)):
                    pool.wait_ge(R2.filled.sem, R2.filled.at(g.ahead(-1), 2))
                normalise(2, g, xhat2, x2[g.parity], xhat2_ready)

            @for_group
            def norm3(g, _):
                small(3, g)

            @for_group
            def bias(g, _):
                if g.first():
                    pool.wait_ge(const_dve, CONST_DVE)
                if counts(O.drained.at(g.ahead(-1), 0)):
                    pool.wait_ge(O.drained.sem, O.drained.at(g.ahead(-1), 0))
                pool.wait_ge(R0.drained.sem, R0.drained.at(g, 10))
                p.tensor_tensor(x1_bias[g.parity][:], x1[g.parity][:],
                                bias1[:].unsqueeze(1).to_broadcast([P, GB, D]), ALU.add)\
                    .then_inc(x1_bias_ready.sem, 1)

            @for_group
            def squares(g, _):
                pool.wait_ge(R0.drained.sem, R0.drained.at(g, 5))
                p.tensor_tensor(relsq[:], relT[:], relT[:], ALU.mult).then_inc(relsq_ready.sem, 1)

            @for_group
            def invert_norm(g, _):
                pool.wait_ge(R0.drained.sem, R0.drained.at(g, 8))
                p.tensor_tensor(rnorm[:], normsq[:], minus_half[:], ALU.pow).then_inc(rnorm_ready.sem, 1)

            @for_group
            def widen_keys(g, m):
                if g.first():
                    pool.wait_ge(const_dve, CONST_DVE)
                pool.wait_ge(R1[m].drained.sem, R1[m].drained.at(g, 2))
                if counts(S.filled.at(g.ahead(-1), 0)):
                    pool.wait_ge(S.filled.sem, S.filled.at(g.ahead(-1), 0))
                apart(pool)
                for h in range(HQ):
                    last = p.tensor_scalar(k_wide[g.parity][:, m, :, h, :], kT[:, m, :].rearrange("p (b n) -> p b n", b=GB),
                                           head_rows[:, h:h + 1], 0.0, ALU.mult, ALU.add)
                last.then_inc(k_wide_ready.sem, 1)

            @for_group
            def normalise_probs(g, u):
                pool.wait_ge(rsums_ready.sem, rsums_ready.at(g, u + 1))
                p.tensor_tensor(probs[:, u % 4, :, :], probs[:, u % 4, :, :],
                                rsums[:, u, :].unsqueeze(2).to_broadcast([P, HQ, N]), ALU.mult)\
                    .then_inc(probs_ready.sem, 1)

            @for_group
            def residual3(g, _):
                pool.wait_ge(gain3_ready.sem, gain3_ready.at(g, 2))
                apart(pool)
                for b in range(GB):
                    p.tensor_scalar(x3[g.parity][:, b, :], x3[g.parity][:, b, :], 1.0, gain3m[:, b:b + 1],
                                    ALU.mult, ALU.add).then_inc(x4_ready.sem, 1)

            normalise0(Group(0, 0))
            pool.wait_ge(const_dve, CONST_TOTAL)
            p.tensor_tensor(w_rnorm[:], w_total[:], minus_half[:, 0:1].to_broadcast([P, len(SCALED)]), ALU.pow)\
                .then_inc(const_pool, 1)
            def iteration(i):
                g0, g1, g2, g3, g4, g5 = (i.ahead(-lag) for lag in range(LAST + 1))
                norm1(g2, 0)

                normalise_probs(g3, 0)
                widen_keys(g3, 1)

                normalise_probs(g3, 1)
                bias(g3, 0)
                squares(g1, 0)

                normalise_probs(g3, 2)
                widen_keys(g2, 0)
                norm3(g5, 0)

                normalise_probs(g3, 3)
                norm2(g4, 0)

                normalise_probs(g3, 4)
                invert_norm(g1, 0)

                normalise_probs(g3, 5)

                normalise_probs(g3, 6)
                norm0(g0, 0)
                residual3(g5, 0)

                normalise_probs(g3, 7)

            iterations(pool, iteration)


CONST_BV, CONST_WA, CONST_TOTAL, CONST_SCALES, CONST_FIRST, CONST_DVE, CONST_POOL = C, 9, 15, 19, 21, 40, 7

_INS = ["x", "adj", "L0_gnn_Wq", "L0_gnn_Wk", "L0_gnn_Wv", "L1_gnn_Wq", "L1_gnn_bq", "L1_gnn_Wk", "L1_gnn_bk",
        "L1_gnn_Wv", "L1_gnn_bv", "L1_gnn_Wo", "L1_gnn_bo", "L2_gnn_W", "L2_gnn_a", "L2_gnn_beta", "L3_gnn_b"]


def kernel(**inputs):
    import concourse.bacc as bacc
    from concourse.bass_utils import run_bass_kernel_spmd

    nc = bacc.Bacc("TRN2", target_bir_lowering=False, num_devices=1)
    arrays, args = {}, []
    for name in _INS:
        a = np.ascontiguousarray(inputs[name])
        arrays[f"in_{name}"] = a
        args.append(nc.dram_tensor(f"in_{name}", a.shape, mybir.dt.from_np(a.dtype), kind="ExternalInput").ap())
    args.append(nc.dram_tensor("out", (B, N, D), F32, kind="ExternalOutput").ap())
    build(nc, *args)
    r = run_bass_kernel_spmd(nc, [arrays], core_ids=[0])
    return r.results[0]["out"]
```
